# Optimizing a Trainium2 kernel written in Bass

```python
import numpy as np
import jax
import jax.numpy as jnp

def _softmax(x, axis=-1):
    return jax.nn.softmax(x, axis=axis)

def _gelu(x):
    return jax.nn.gelu(x, approximate=True)

def _silu(x):
    return jax.nn.silu(x)

def _sigmoid(x):
    return jax.nn.sigmoid(x)

def _layernorm(x, axis=-1, eps=1e-05):
    m = jnp.mean(x, axis=axis, keepdims=True)
    v = jnp.var(x, axis=axis, keepdims=True)
    return (x - m) / jnp.sqrt(v + eps)

def _scatter_add(tgt, idx, src, axis=0):
    return tgt.at[idx].add(src)

def _segment_sum(src, seg, n):
    return jax.ops.segment_sum(src, seg, n)
kernel_name = 'mk_adj_preln_d2_adj_r2_84e081'

def setup_inputs(seed: int=0):
    np.random.seed(seed)
    _w = jnp.asarray

    def _rec_inputs():
        import jax
        import jax.numpy as jnp
        _gk = jax.random.key(seed)
        x = -0.000929 + 1 * jax.random.normal(jax.random.fold_in(_gk, 1), (32, 256, 256), jnp.float32)
        _a = jax.random.bernoulli(jax.random.fold_in(_gk, 2), 0.0625, (256, 256))
        adj = _a.astype(jnp.int32)
        return (x, adj)
    x, adj = _rec_inputs()

    def _L0_gnn_setup():
        import jax, jax.numpy as jnp
        import numpy as np
        B, K, DIN, DOUT = (32, 64, 256, 256)
        key = jax.random.key(seed)
        k1, k2, k3, k4 = jax.random.split(key, 4)
        x = jax.random.normal(k1, (B, K, DIN), dtype=jnp.float32)
        adj = jax.random.randint(k2, (K, K), 0, 2, dtype=jnp.int32)
        W = jax.random.normal(k3, (DOUT, 2 * DIN), dtype=jnp.float32) * 0.02
        b = jax.random.normal(k4, (DOUT,), dtype=jnp.float32) * 0.02
        return {'x': x, 'adj': adj, 'W': W, 'b': b}
    _L0_gnn_all = _L0_gnn_setup()
    _L0_gnn_in = {k: v for k, v in _L0_gnn_all.items() if k in ('W', 'b')}
    del _L0_gnn_all

    def _L1_gnn_setup():
        import jax, jax.numpy as jnp
        import numpy as np
        LEAKY_ALPHA = 0.01
        NEG_INF = -1000000000.0
        LN_EPS = 1e-05

        def _gat_heads(x, adj, W, a):
            O = W.shape[-1]
            Wh = jnp.einsum('bnf,hfo->bhno', x, W)
            f1 = jnp.einsum('bhno,ho->bhn', Wh, a[:, :O])
            f2 = jnp.einsum('bhno,ho->bhn', Wh, a[:, O:])
            e = f1[:, :, :, None] + f2[:, :, None, :]
            e = jnp.where(e > 0, e, LEAKY_ALPHA * e)
            e = jnp.where(adj[None, None] > 0, e, NEG_INF)
            attn = jax.nn.softmax(e, axis=-1)
            return jnp.einsum('bhnm,bhmo->bhno', attn, Wh)
        key = jax.random.key(seed)
        ks = jax.random.split(key, 10)
        B, N, F_in, F_hid, H, F_out, D_ff = (8, 1024, 256, 256, 4, 256, 256)
        s = 0.05
        return {'enc_inputs': jax.random.normal(ks[0], (B, N, F_in), jnp.float32), 'adj': jax.random.randint(ks[1], (N, N), 0, 2, jnp.int32), 'W_heads': jax.random.normal(ks[2], (H, F_in, F_hid), jnp.float32) * s, 'a_heads': jax.random.normal(ks[3], (H, 2 * F_hid), jnp.float32) * s, 'W_out': jax.random.normal(ks[4], (H * F_hid, F_out), jnp.float32) * s, 'a_out': jax.random.normal(ks[5], (2 * F_out,), jnp.float32) * s, 'w1': jax.random.normal(ks[6], (F_out, D_ff), jnp.float32) * s, 'b1': jnp.zeros((D_ff,), jnp.float32), 'w2': jax.random.normal(ks[7], (D_ff, F_out), jnp.float32) * s, 'b2': jnp.zeros((F_out,), jnp.float32), 'ln_gamma': jnp.ones((F_out,), jnp.float32), 'ln_beta': jnp.zeros((F_out,), jnp.float32)}
    _L1_gnn_all = _L1_gnn_setup()
    _L1_gnn_in = {k: v for k, v in _L1_gnn_all.items() if k in ('W_heads', 'a_heads', 'W_out', 'a_out', 'w1', 'b1', 'w2', 'b2', 'ln_gamma', 'ln_beta')}
    del _L1_gnn_all
    return {'x': x, 'adj': adj, 'L0_gnn_W': _L0_gnn_in['W'], 'L0_gnn_b': _L0_gnn_in['b'], 'L1_gnn_W_heads': _L1_gnn_in['W_heads'], 'L1_gnn_a_heads': _L1_gnn_in['a_heads'], 'L1_gnn_W_out': _L1_gnn_in['W_out'], 'L1_gnn_a_out': _L1_gnn_in['a_out'], 'L1_gnn_w1': _L1_gnn_in['w1'], 'L1_gnn_b1': _L1_gnn_in['b1'], 'L1_gnn_w2': _L1_gnn_in['w2'], 'L1_gnn_b2': _L1_gnn_in['b2'], 'L1_gnn_ln_gamma': _L1_gnn_in['ln_gamma'], 'L1_gnn_ln_beta': _L1_gnn_in['ln_beta']}

def reference(x, adj, L0_gnn_W, L0_gnn_b, L1_gnn_W_heads, L1_gnn_a_heads, L1_gnn_W_out, L1_gnn_a_out, L1_gnn_w1, L1_gnn_b1, L1_gnn_w2, L1_gnn_b2, L1_gnn_ln_gamma, L1_gnn_ln_beta):
    import jax
    import jax.numpy as jnp

    def _L0_gnn_ref(x, adj, W, b):
        import jax, jax.numpy as jnp
        import numpy as np
        B, K, DIN, DOUT = (32, 64, 256, 256)
        Din = x.shape[-1]
        Wi, Wj = (W[:, :Din], W[:, Din:])
        mi = jnp.einsum('bkd,od->bko', x, Wi)
        mj = jnp.einsum('bkd,od->bko', x, Wj)
        a = adj.astype(x.dtype)
        deg = a.sum(axis=1)
        out = deg[None, :, None] * (mi + b) + jnp.einsum('ij,bjo->bio', a, mj)
        return out

    def _L1_gnn_ref(enc_inputs, adj, W_heads, a_heads, W_out, a_out, w1, b1, w2, b2, ln_gamma, ln_beta):
        import jax, jax.numpy as jnp
        import numpy as np
        LEAKY_ALPHA = 0.01
        NEG_INF = -1000000000.0
        LN_EPS = 1e-05

        def _gat_heads(x, adj, W, a):
            O = W.shape[-1]
            Wh = jnp.einsum('bnf,hfo->bhno', x, W)
            f1 = jnp.einsum('bhno,ho->bhn', Wh, a[:, :O])
            f2 = jnp.einsum('bhno,ho->bhn', Wh, a[:, O:])
            e = f1[:, :, :, None] + f2[:, :, None, :]
            e = jnp.where(e > 0, e, LEAKY_ALPHA * e)
            e = jnp.where(adj[None, None] > 0, e, NEG_INF)
            attn = jax.nn.softmax(e, axis=-1)
            return jnp.einsum('bhnm,bhmo->bhno', attn, Wh)
        B, N, _ = enc_inputs.shape
        h = jax.nn.elu(_gat_heads(enc_inputs, adj, W_heads, a_heads))
        h = jnp.transpose(h, (0, 2, 1, 3)).reshape(B, N, -1)
        out = _gat_heads(h, adj, W_out[None], a_out[None])[:, 0]
        out = jax.nn.elu(out)
        ffn = jnp.maximum(out @ w1 + b1, 0.0) @ w2 + b2
        y = ffn + out
        mu = jnp.mean(y, axis=-1, keepdims=True)
        var = jnp.var(y, axis=-1, keepdims=True)
        return (y - mu) / jnp.sqrt(var + LN_EPS) * ln_gamma + ln_beta
    h = jnp.maximum(_layernorm(x, axis=-1), 0.0)
    x = x + _L0_gnn_ref(h, adj, L0_gnn_W, L0_gnn_b)
    h = jnp.maximum(_layernorm(x, axis=-1), 0.0)
    x = x + _L1_gnn_ref(h, adj, L1_gnn_W_heads, L1_gnn_a_heads, L1_gnn_W_out, L1_gnn_a_out, L1_gnn_w1, L1_gnn_b1, L1_gnn_w2, L1_gnn_b2, L1_gnn_ln_gamma, L1_gnn_ln_beta)
    return x

_drawn_inputs = setup_inputs


def setup_inputs(seed=0):
    import zlib

    import numpy as np

    out = dict(_drawn_inputs(seed))
    spreads = {'L1_gnn_b1': (0.0, 0.395),
     'L1_gnn_b2': (0.0, 0.1),
     'L1_gnn_ln_gamma': (1.0, 0.2),
     'L1_gnn_ln_beta': (0.0, 0.386)}
    factors = {'L1_gnn_a_heads': 8.0, 'L1_gnn_a_out': 8.0}
    for name, (base, spread) in spreads.items():
        noise = np.random.default_rng([zlib.crc32(name.encode()), seed]).standard_normal(out[name].shape)
        drawn = base * np.exp(spread * noise) if base else spread * noise
        out[name] = jnp.asarray(drawn.astype(out[name].dtype))
    for name, factor in factors.items():
        out[name] = (out[name] * factor).astype(out[name].dtype)
    return out
```

```python
import concourse.bass as bass
from concourse import mybir
from contextlib import ExitStack


def gnn_block_kernel(nc, x, adj, l0_w, l0_b, w_heads, a_heads, w_out, a_out, w1, b1, w2, b2, gamma, beta, out):
    F32 = mybir.dt.float32
    F32R = mybir.dt.float32r
    I32 = mybir.dt.int32
    ALU = mybir.AluOpType
    ACT = mybir.ActivationFunctionType
    AX = mybir.AxisListType

    P = 128
    BATCHES, N, D = x.shape
    H = w_heads.shape[0]
    NT = N // P
    DT = D // P
    LAST = H
    NF = 2 * H
    WVN = NF + H * D
    CHUNKS = 3
    CW = WVN // CHUNKS
    W2N = D + 2
    KT = H * DT
    MASKED = -1e11
    SLOPE = 0.01
    EPS = 1e-5
    assert CHUNKS * CW == WVN and CW <= 512 and NT == 2 and DT == 2 and NT * D == 512

    with ExitStack() as ctx:
        def sb(name, shape, dt=F32):
            return ctx.enter_context(nc.sbuf_tensor(name, shape, dt))

        def sem(name):
            return ctx.enter_context(nc.semaphore(name))

        def split(name, shape):
            return sb(name + "_hi", shape, F32R), sb(name + "_lo", shape, F32R)

        ident = sb("ident", [P, P])
        neg_half = sb("neg_half", [P, NT])
        adj_i = sb("adj_i", [P, NT, N], I32)
        adj_f = sb("adj_f", [P, NT, N])
        deg = sb("deg", [P, NT])
        mask = sb("mask", [P, NT, N])
        ad = sb("ad", [P, 768])
        ad_s = split("ad", [P, 768])
        w_l0 = sb("w_l0", [P, DT, 2 * D])
        wij_s = split("wij", [P, 2 * DT, D])
        b_l0 = sb("b_l0", [P, D])
        deg_b = sb("deg_b", [P, NT, D])
        wv_s = split("wv", [P, DT, WVN])
        wo_s = split("wo", [P, KT, W2N])
        w1_s = split("w1", [P, DT, D])
        w2_s = split("w2", [P, DT, D])
        b1_c = sb("b1_c", [P, DT])
        b2_r = sb("b2_r", [P, NT, D])
        gamma_r = sb("gamma_r", [P, NT, D])
        beta_r = sb("beta_r", [P, NT, D])
        junk = sb("junk", [P, 2, D])

        x_t = sb("x_t", [P, NT, D])
        xdb = sb("xdb", [P, NT, D])
        st1, st2, st3 = (sb(f"st{i}", [P, NT, 6]) for i in (1, 2, 3))
        mv1, mv2, mv3 = (sb(f"mv{i}", [P, NT, 2]) for i in (1, 2, 3))
        ve1, ve2, ve3 = (sb(f"ve{i}", [P, NT]) for i in (1, 2, 3))
        rs1, rs2, rs3 = (sb(f"rs{i}", [P, NT]) for i in (1, 2, 3))
        nb1, nb2, nb3 = (sb(f"nb{i}", [P, NT]) for i in (1, 2, 3))
        h_f = sb("h_f", [P, NT, D])
        h_s = split("h", [P, NT, D])
        g_s = split("g", [P, DT, 512])
        x1a = sb("x1a", [P, NT, D])
        x1b = sb("x1b", [P, NT, D])
        x1c = sb("x1c", [P, NT, D])
        h2 = sb("h2", [P, NT, D])
        h2t_s = split("h2t", [P, DT, N])

        whv = sb("whv", [P, NT, WVN])
        wh2 = sb("wh2", [P, NT, W2N])
        f1s = sb("f1s", [P, NT, H])
        f1s4 = sb("f1s4", [P, NT, 1])
        m2 = sb("m2", [P, NT, H])
        m24 = sb("m24", [P, NT, 1])
        nsum = sb("nsum", [P, NT, H])
        nsum4 = sb("nsum4", [P, NT, 1])
        negm = sb("negm", [P, NT, H])
        negm4 = sb("negm4", [P, NT, 1])
        z = [sb(f"z{h}", [P, NT, N]) for h in range(H + 1)]
        lw = [sb(f"lw{h}", [P, NT, N]) for h in range(H + 1)]
        p = [sb(f"p{h}", [P, NT, N]) for h in range(H + 1)]
        rsum = [sb(f"rsum{h}", [P, NT]) for h in range(H + 1)]
        rinv = [sb(f"rinv{h}", [P, NT]) for h in range(H + 1)]
        pt_all = sb("pt_all", [P, H + 1, NT * N])
        hh_all = sb("hh_all", [P, H + 1, NT * D])
        pt = [pt_all[:, h, :].rearrange("p (t n) -> p t n", t=NT) for h in range(H + 1)]
        hh = [hh_all[:, h, :].rearrange("p (t n) -> p t n", t=NT) for h in range(H + 1)]
        wv = whv
        wo = pt_all[:, :, :].rearrange("p h n -> p (h n)")[:, 0:KT * W2N].rearrange("p (k n) -> p k n", k=KT)
        a_h = hh_all[:, 0:H, :]
        w1_f, w2_f = z[0], z[1]
        a_o = z[2][:, :, :].rearrange("p t n -> p (t n)")
        ht_s = split("ht", [P, KT, N])
        ot_s = split("ot", [P, DT, N])
        ob2 = sb("ob2", [P, NT, D])
        ff = sb("ff", [P, DT, N])
        ff_s = split("ff", [P, DT, N])
        y = sb("y", [P, NT, D])
        yn = sb("yn", [P, NT, D])
        yg = sb("yg", [P, NT, D])
        o_t = sb("o_t", [P, NT, D])

        bank = ctx.enter_context(nc.psum_tensor("bank", [P, 8, 512], F32))

        def tiles(k):
            return bank[:, k, :].rearrange("p (t n) -> p t n", t=2)

        adj_in, l0_in, heads_in, out_in, ffn_in, rows_in = (
            sem(n) for n in ("adj_in", "l0_in", "heads_in", "out_in", "ffn_in", "rows_in"))
        ident_zero, ident_ready, half_ready = sem("ident_zero"), sem("ident_ready"), sem("half_ready")
        adj_cast, deg_ready, mask_ready, adt_psum, adt_ready, diag_ready, ad_hi_ready, ad_ready = (
            sem(n) for n in ("adj_cast", "deg_ready", "mask_ready", "adt_psum", "adt_ready", "diag_ready",
                             "ad_hi_ready", "ad_ready"))
        wt_psum, wij_hi_ready, wij_ready, deg_b_ready = (
            sem(n) for n in ("wt_psum", "wij_hi_ready", "wij_ready", "deg_b_ready"))
        wv_full, wv_hi_ready, wv_ready, wo_full, wo_hi_ready, wo_ready, ffn_hi_ready, ffn_ready = (
            sem(n) for n in ("wv_full", "wv_hi_ready", "wv_ready", "wo_full", "wo_hi_ready", "wo_ready",
                             "ffn_hi_ready", "ffn_ready"))
        x_loaded, xdb_ready = sem("x_loaded"), sem("xdb_ready")
        stats1, moments1, var1, rstd1, bias1 = (sem(n + "1") for n in ("stats", "moments", "var", "rstd", "bias"))
        stats2, moments2, var2, rstd2, bias2 = (sem(n + "2") for n in ("stats", "moments", "var", "rstd", "bias"))
        stats3, moments3, var3, rstd3, bias3 = (sem(n + "3") for n in ("stats", "moments", "var", "rstd", "bias"))
        h_full, h_hi, h_lo, sums_psum, g_hi, g_lo = (
            sem(n) for n in ("h_full", "h_hi_done", "h_lo_done", "sums_psum", "g_hi_done", "g_lo_done"))
        x1_psum, x1_ready, x1_kept, x1_beta, h2_ready, h2t_psum, h2t_hi, h2t_lo = (
            sem(n) for n in ("x1_psum", "x1_ready", "x1_kept", "x1_beta", "h2_ready", "h2t_psum",
                             "h2t_hi_done", "h2t_lo_done"))
        wh_psum = [sem(f"wh_psum{c}") for c in range(CHUNKS)]
        wh_sb = [sem(f"wh_sb{c}") for c in range(CHUNKS)]
        wh2_psum, wh2_sb, f1_scaled, f14_scaled = (sem(n) for n in ("wh2_psum", "wh2_sb", "f1_scaled", "f14_scaled"))
        rows_psum = [sem(f"rows_psum{k}") for k in range(3)]
        z_ready = [sem(f"z_ready{k}") for k in range(3)]
        nsum_ready, nsum4_ready, negm_ready, negm4_ready = (
            sem(n) for n in ("nsum_ready", "nsum4_ready", "negm_ready", "negm4_ready"))
        per_head = ("lw_ready", "le_ready", "p_ready", "pt_psum", "pt_ready", "pv_psum", "ex_ready", "rinv_ready",
                    "em_ready", "hh_ready")
        (lw_ready, le_ready, p_ready, pt_psum, pt_ready, pv_psum, ex_ready, rinv_ready, em_ready, hh_ready) = (
            [sem(f"{n}{h}") for h in range(H + 1)] for n in per_head)
        ht_psum, ht_hi, ht_lo = ([sem(f"{n}{h}") for h in range(H)] for n in ("ht_psum", "ht_hi_done", "ht_lo_done"))
        ot_psum, ot_hi, ot_lo, ob2_ready, f_psum, f_full, f_hi, f_lo, y_psum, y_ready, yn_ready, yg_ready = (
            sem(n) for n in ("ot_psum", "ot_hi_done", "ot_lo_done", "ob2_ready", "f_psum", "f_full", "f_hi_done",
                             "f_lo_done", "y_psum", "y_ready", "yn_ready", "yg_ready"))
        out_ready, out_stored = sem("out_ready"), sem("out_stored")

        def counts(eng, t, lags=(0, 1, 2, 3)):
            if isinstance(t, int):
                return {k: max(0, min(BATCHES, t + 1 - k)) for k in lags}
            return {k: eng.snap(t + 1 - k) for k in lags}

        def turns(eng, turn):
            turn(0, True, False, False)
            turn(1, True, True, False)
            turn(2, True, True, True)
            with eng.Fori(3, BATCHES) as t:
                turn(t, True, True, True)
            turn(BATCHES, False, True, True)
            turn(BATCHES + 1, False, False, True)

        block = ctx.enter_context(nc.Block())

        @block.sync
        def _(sp):
            sp.dma_start(adj_i[:, :, :], adj.rearrange("(t p) m -> p t m", p=P)).then_inc(adj_in, 16)
            sp.dma_start(w_l0[:, :, :], l0_w.rearrange("(t p) d -> p t d", p=P)).then_inc(l0_in, 16)
            sp.dma_start(b_l0[:, :], l0_b.partition_broadcast(P)).then_inc(l0_in, 16)
            sp.dma_start(x_t[:, :, :], x[0].rearrange("(t p) d -> p t d", p=P)).then_inc(x_loaded, 16)
            sp.dma_start(a_h[:, :, :], a_heads.partition_broadcast(P)).then_inc(heads_in, 16)
            for h in range(H):
                sp.dma_start(wv[:, :, NF + h * D:NF + (h + 1) * D],
                             w_heads[h].rearrange("(t p) o -> p t o", p=P)).then_inc(heads_in, 16)
            sp.dma_start(a_o[:, :], a_out.partition_broadcast(P)).then_inc(out_in, 16)
            sp.dma_start(wo[:, :, 0:D], w_out.rearrange("(t p) o -> p t o", p=P)).then_inc(out_in, 16)
            sp.dma_start(w1_f[:, :, :], w1.rearrange("(t p) o -> p t o", p=P)).then_inc(ffn_in, 16)
            sp.dma_start(w2_f[:, :, :], w2.rearrange("(t p) o -> p t o", p=P)).then_inc(ffn_in, 16)
            with nc.allow_non_contiguous_dma("one column of biases"):
                sp.dma_start(b1_c[:, :], b1.rearrange("(t p) -> p t", p=P)).then_inc(rows_in, 16)
            for row, vec in ((b2_r, b2), (gamma_r, gamma), (beta_r, beta)):
                for t in range(NT):
                    sp.dma_start(row[:, t, :], vec.partition_broadcast(P)).then_inc(rows_in, 16)

            def load(b, n):
                sp.wait_ge(xdb_ready, n)
                sp.wait_ge(h_full, n)
                sp.dma_start(x_t[:, :, :], x[b].rearrange("(t p) d -> p t d", p=P)).then_inc(x_loaded, 16)

            def store(b, n):
                sp.wait_ge(out_ready, n)
                sp.dma_start(out[b].rearrange("(t p) d -> p t d", p=P), o_t[:, :, :]).then_inc(out_stored, 16)

            load(1, 1)
            load(2, 2)
            with sp.Fori(3, BATCHES) as t:
                n_loaded, n_out = sp.snap(t + 0), sp.snap(t - 2)
                load(t, n_loaded)
                store(t - 3, n_out)
            for b in range(BATCHES - 3, BATCHES):
                store(b, b + 1)
            sp.wait_ge(out_stored, 16 * BATCHES)

        @block.gpsimd
        def _(pool):
            nc.gpsimd.memset(ident[:, :], 0.0).then_inc(ident_zero, 1)
            nc.gpsimd.memset(neg_half[:, :], -0.5).then_inc(half_ready, 1)
            pool.wait_ge(ident_zero, 1)
            nc.gpsimd.affine_select(out=ident[:, :], in_=ident[:, :], compare_op=ALU.not_equal, fill=1.0, base=0,
                                    pattern=[[-1, P]], channel_multiplier=1).then_inc(ident_ready, 1)
            pool.wait_ge(half_ready, 1)

            def turn(t, stage_b, stage_c, stage_d):
                now = counts(pool, t)
                if stage_b:
                    pool.wait_ge(var1, now[0])
                    pool.wait_ge(bias1, now[1])
                    nc.gpsimd.tensor_tensor(rs1[:, :], ve1[:, :], neg_half[:, :], ALU.pow).then_inc(rstd1, 1)
                    pool.wait_ge(deg_b_ready, NT)
                    pool.wait_ge(x1_ready, now[1])
                    nc.gpsimd.tensor_tensor(xdb[:, :, :], x_t[:, :, :], deg_b[:, :, :], ALU.add).then_inc(xdb_ready, 1)
                if stage_d:
                    pool.wait_ge(rows_in, 7 * 16)
                    pool.wait_ge(out_ready, now[3])
                    pool.wait_ge(x1_kept, now[2])
                    nc.gpsimd.tensor_tensor(x1c[:, :, :], x1b[:, :, :], beta_r[:, :, :], ALU.add).then_inc(x1_beta, 1)
                if stage_b:
                    pool.wait_ge(sums_psum, now[1])
                    pool.wait_ge(h_hi, now[0])
                    nc.gpsimd.tensor_tensor(h_s[1][:, :, :], h_f[:, :, :], h_s[0][:, :, :].bitcast(F32),
                                            ALU.subtract).then_inc(h_lo, 1)
                if stage_d:
                    pool.wait_ge(y_ready, now[3])
                    pool.wait_ge(hh_ready[LAST], now[2])
                    nc.gpsimd.tensor_tensor(ob2[:, :, :], hh[LAST][:, :, :], b2_r[:, :, :], ALU.add).then_inc(ob2_ready, 1)
                if stage_b:
                    pool.wait_ge(bias2, now[1])
                    pool.wait_ge(var2, now[0])
                    nc.gpsimd.tensor_tensor(rs2[:, :], ve2[:, :], neg_half[:, :], ALU.pow).then_inc(rstd2, 1)
                if stage_d:
                    pool.wait_ge(y_psum, now[3])
                    pool.wait_ge(f_hi, now[2])
                    nc.gpsimd.tensor_tensor(ff_s[1][:, :, :], ff[:, :, :], ff_s[0][:, :, :].bitcast(F32),
                                            ALU.subtract).then_inc(f_lo, 1)
                    pool.wait_ge(yn_ready, now[3])
                    pool.wait_ge(var3, now[2])
                    nc.gpsimd.tensor_tensor(rs3[:, :], ve3[:, :], neg_half[:, :], ALU.pow).then_inc(rstd3, 1)
                    pool.wait_ge(yn_ready, now[2])
                    nc.gpsimd.tensor_tensor(yg[:, :, :], yn[:, :, :], gamma_r[:, :, :], ALU.mult).then_inc(yg_ready, 1)
                    pool.wait_ge(yg_ready, now[2])
                    stored = 16 * now[3] if isinstance(t, int) else pool.snap(16 * t - 32)
                    pool.wait_ge(out_stored, stored)
                    nc.gpsimd.tensor_tensor(o_t[:, :, :], yg[:, :, :], x1c[:, :, :], ALU.add).then_inc(out_ready, 1)

            turns(pool, turn)

        @block.tensor
        def _(pe):
            def product(dst, terms):
                passes = [(l[i], r[j]) for l, r in terms
                          for i, j in ([(0, 0)] if len(l) == 1 else [(0, 0), (0, 1), (1, 0)])]
                for n, (lhs, rhs) in enumerate(passes):
                    last = nc.tensor.matmul(dst, lhs, rhs, start=(n == 0), stop=(n == len(passes) - 1))
                return last

            def parts(s, *index):
                return tuple(q[index] for q in s)

            def turn_over(dst, src):
                for i in range(2):
                    for j in range(2):
                        last = nc.tensor.transpose(dst[:, j, i * P:(i + 1) * P], src[:, i, j * P:(j + 1) * P], ident[:, :])
                return last

            pe.wait_ge(ident_ready, 1)
            pe.wait_ge(adj_cast, 1)
            turn_over(tiles(0), adj_f).then_inc(adt_psum, 1)
            pe.wait_ge(l0_in, 2 * 16)
            for k in range(2):
                last = turn_over(tiles(1 + k), w_l0[:, :, k * D:(k + 1) * D])
            last.then_inc(wt_psum, 1)

            def rows(dst, f2):
                for k in range(NT):
                    last = nc.tensor.transpose(dst[:, k * P:(k + 1) * P], f2[:, k, :].to_broadcast([P, P]), ident[:, :])
                return last

            def attend(k, h, values):
                for i in range(NT):
                    last = product(tiles(k)[:, i, :], [((pt[h][:, j, i * P:(i + 1) * P],), (values(j),))
                                                       for j in range(NT)])
                return last

            def turn(t, stage_b, stage_c, stage_d):
                now = counts(pe, t)
                nk = KT - DT

                def layer2(i, ks):
                    for k in ks:
                        for a, b in ((0, 0), (0, 1), (1, 0)):
                            last = nc.tensor.matmul(bank[:, i, 0:W2N], ht_s[a][:, k, i * P:(i + 1) * P], wo_s[b][:, k, :],
                                                    start=(k == 0 and (a, b) == (0, 0)), stop=(k == KT - 1 and (a, b) == (1, 0)))
                    return last

                def heads(c, k):
                    for i in range(NT):
                        last = product(bank[:, k + i, 0:CW], [(parts(h2t_s, slice(None), f, slice(i * P, (i + 1) * P)),
                                                               parts(wv_s, slice(None), f, slice(c * CW, (c + 1) * CW)))
                                                              for f in range(DT)])
                    return last

                if stage_d:
                    pe.wait_ge(wo_ready, 1)
                    for h in range(H - 1):
                        pe.wait_ge(ht_lo[h], now[2])
                    pe.wait_ge(hh_ready[2], now[2])
                    for i in range(NT):
                        layer2(i, range(nk))
                    pe.wait_ge(h2t_lo, now[1])
                    pe.wait_ge(hh_ready[3], now[2])
                    turn_over(tiles(4), hh[3]).then_inc(ht_psum[3], 1)
                if stage_c:
                    pe.wait_ge(wv_ready, 1)
                    pe.wait_ge(h2t_lo, now[1])
                    pe.wait_ge(ht_lo[2], now[2])
                    pe.wait_ge(ht_lo[0], now[2])
                    heads(0, 2).then_inc(wh_psum[0], 1)
                if stage_d:
                    pe.wait_ge(ht_lo[3], now[2])
                    for i in range(NT):
                        last = layer2(i, range(nk, KT))
                    last.then_inc(wh2_psum, 1)
                if stage_c:
                    pe.wait_ge(wh_sb[0], now[1])
                    pe.wait_ge(ht_lo[3], now[2])
                    for h in (0, 1):
                        last = rows(tiles(4)[:, h, :], whv[:, :, H + h:H + h + 1])
                    last.then_inc(rows_psum[0], 1)
                    pe.wait_ge(y_ready, now[3])
                    for h in (2, 3):
                        last = rows(tiles(5)[:, h - 2, :], whv[:, :, H + h:H + h + 1])
                    last.then_inc(rows_psum[1], 1)
                    pe.wait_ge(pt_ready[3], now[2])
                    pe.wait_ge(hh_ready[3], now[2])
                    heads(1, 6).then_inc(wh_psum[1], 1)
                if stage_d:
                    pe.wait_ge(wh_sb[0], now[1])
                    pe.wait_ge(wh2_sb, now[2])
                    rows(tiles(2)[:, 0, :], wh2[:, :, D + 1:D + 2]).then_inc(rows_psum[2], 1)
                if stage_c:
                    pe.wait_ge(wh2_sb, now[2])
                    heads(2, 0).then_inc(wh_psum[2], 1)
                if stage_b:
                    pe.wait_ge(ad_ready, 1)
                    pe.wait_ge(wh_sb[1], now[1])
                    pe.wait_ge(h_lo, now[0])
                    for d in range(DT):
                        for n, (dst, cols) in enumerate(((slice(0, 384), slice(0, 384)), (slice(128, 512), slice(384, 768)))):
                            for m, (a, b) in enumerate(((0, 0), (0, 1), (1, 0))):
                                last = nc.tensor.matmul(bank[:, 6 + d, dst], h_s[a][:, n, d * P:(d + 1) * P],
                                                        ad_s[b][:, cols], start=(n == 0 and m == 0),
                                                        stop=(n == 1 and m == 2), skip_group_check=True)
                    last.then_inc(sums_psum, 1)
                if stage_d:
                    pe.wait_ge(wh_sb[0], now[1])
                    pe.wait_ge(p_ready[LAST], now[2])
                    turn_over(tiles(3), p[LAST]).then_inc(pt_psum[LAST], 1)
                if stage_c:
                    pe.wait_ge(z_ready[2], now[2])
                    pe.wait_ge(p_ready[0], now[1])
                    turn_over(tiles(2), p[0]).then_inc(pt_psum[0], 1)
                if stage_d:
                    pe.wait_ge(wh_sb[2], now[1])
                    pe.wait_ge(pt_ready[LAST], now[2])
                    attend(0, LAST, lambda j: wh2[:, j, 0:D]).then_inc(pv_psum[LAST], 1)

                def head_out(h, k):
                    attend(k, h, lambda j: whv[:, j, NF + h * D:NF + (h + 1) * D]).then_inc(pv_psum[h], 1)

                if stage_c:
                    pe.wait_ge(wh_sb[2], now[1])
                    pe.wait_ge(pt_ready[0], now[1])
                    head_out(0, 1)
                if stage_b:
                    pe.wait_ge(wij_ready, 1)
                    pe.wait_ge(z_ready[0], now[1])
                    pe.wait_ge(g_lo, now[0])
                    for i, (d0, a0) in enumerate(((0, 128), (384, 256))):
                        last = product(tiles(4)[:, i, :],
                                       [(parts(g_s, slice(None), f, slice(c0, c0 + P)),
                                         parts(wij_s, slice(None), s * DT + f, slice(None)))
                                        for s, c0 in enumerate((d0, a0)) for f in range(DT)])
                    last.then_inc(x1_psum, 1)
                if stage_c:
                    pe.wait_ge(z_ready[1], now[1])
                    pe.wait_ge(p_ready[1], now[1])
                    turn_over(tiles(5), p[1]).then_inc(pt_psum[1], 1)
                if stage_d:
                    pe.wait_ge(pt_ready[LAST], now[2])
                    pe.wait_ge(hh_ready[LAST], now[2])
                    turn_over(tiles(3), hh[LAST]).then_inc(ot_psum, 1)
                if stage_c:
                    pe.wait_ge(pt_ready[0], now[1])
                    pe.wait_ge(pt_ready[1], now[1])
                    head_out(1, 2)
                if stage_d:
                    pe.wait_ge(ffn_ready, 2)
                    pe.wait_ge(g_lo, now[0])
                    pe.wait_ge(ot_lo, now[2])
                    for i in range(DT):
                        last = product(tiles(6)[:, i, :], [(parts(w1_s, slice(None), f, slice(i * P, (i + 1) * P)),
                                                            parts(ot_s, slice(None), f, slice(None))) for f in range(DT)])
                    last.then_inc(f_psum, 1)
                if stage_c:
                    pe.wait_ge(g_lo, now[0])
                    pe.wait_ge(p_ready[2], now[1])
                    turn_over(tiles(7), p[2]).then_inc(pt_psum[2], 1)
                    pe.wait_ge(ot_lo, now[2])
                    pe.wait_ge(hh_ready[0], now[1])
                    turn_over(tiles(3), hh[0]).then_inc(ht_psum[0], 1)
                    pe.wait_ge(hh_ready[LAST], now[2])
                    pe.wait_ge(pt_ready[2], now[1])
                    head_out(2, 0)
                if stage_d:
                    pe.wait_ge(pt_ready[1], now[1])
                    pe.wait_ge(f_lo, now[2])
                    for i in range(NT):
                        last = product(tiles(5)[:, i, :], [(parts(ff_s, slice(None), f, slice(i * P, (i + 1) * P)),
                                                            parts(w2_s, slice(None), f, slice(None))) for f in range(DT)])
                    last.then_inc(y_psum, 1)
                if stage_c:
                    pe.wait_ge(f_full, now[2])
                    pe.wait_ge(p_ready[3], now[1])
                    turn_over(tiles(6), p[3]).then_inc(pt_psum[3], 1)
                    pe.wait_ge(hh_ready[1], now[1])
                    turn_over(tiles(1), hh[1]).then_inc(ht_psum[1], 1)
                if stage_b:
                    pe.wait_ge(x1_ready, now[0])
                    pe.wait_ge(h2_ready, now[0])
                    turn_over(tiles(4), h2).then_inc(h2t_psum, 1)
                if stage_c:
                    pe.wait_ge(pt_ready[2], now[1])
                    pe.wait_ge(pt_ready[3], now[1])
                    head_out(3, 7)
                    pe.wait_ge(hh_ready[2], now[1])
                    turn_over(tiles(2), hh[2]).then_inc(ht_psum[2], 1)

            turns(pe, turn)

        @block.scalar
        def _(act):
            def turn(t, stage_b, stage_c, stage_d):
                now = counts(act, t)
                lag = [1] * H + [2]

                def chunk(c, k):
                    act.wait_ge(wh_psum[c], now[1])
                    nc.scalar.activation(whv[:, :, c * CW:(c + 1) * CW], bank[:, k:k + 2, 0:CW],
                                         ACT.Copy).then_inc(wh_sb[c], 1)

                def slope(h):
                    if h == LAST:
                        act.wait_ge(f14_scaled, now[2])
                        act.wait_ge(z_ready[2], now[2])
                    else:
                        act.wait_ge(f1_scaled, now[1])
                        act.wait_ge(z_ready[h // 2], now[1])
                    for i in range(NT):
                        f = f1s4[:, i, 0:1] if h == LAST else f1s[:, i, h:h + 1]
                        last = nc.scalar.activation(lw[h][:, i, :], z[h][:, i, :], ACT.Identity, bias=f, scale=SLOPE)
                    last.then_inc(lw_ready[h], 1)

                def probs(h):
                    act.wait_ge(negm4_ready if h == LAST else negm_ready, now[lag[h]])
                    act.wait_ge(hh_ready[h], now[lag[h] + 1])
                    act.wait_ge(rinv_ready[h], now[lag[h] + 1])
                    act.wait_ge(le_ready[h], now[lag[h]])
                    for i in range(NT):
                        m = negm4[:, i, 0:1] if h == LAST else negm[:, i, h:h + 1]
                        last = nc.scalar.activation(p[h][:, i, :], lw[h][:, i, :], ACT.Exp, bias=m,
                                                    accum_out=rsum[h][:, i:i + 1])
                    last.then_inc(p_ready[h], 1)

                def keep_pt(h, k):
                    act.wait_ge(pt_psum[h], now[lag[h]])
                    nc.scalar.activation(pt[h][:, :, :], tiles(k), ACT.Copy).then_inc(pt_ready[h], 1)

                def elu_exp(h, k):
                    act.wait_ge(rinv_ready[h], now[lag[h]])
                    act.wait_ge(pv_psum[h], now[lag[h]])
                    for i in range(NT):
                        last = nc.scalar.activation(p[h][:, i, :], tiles(k)[:, i, :], ACT.Exp, scale=rinv[h][:, i:i + 1])
                    last.then_inc(ex_ready[h], 1)

                def keep_ht(h, k, n):
                    act.wait_ge(ht_psum[h], n)
                    nc.scalar.activation(ht_s[0][:, DT * h:DT * h + DT, :], tiles(k), ACT.Copy).then_inc(ht_hi[h], 1)

                if stage_b:
                    act.wait_ge(h_lo, now[1])
                    act.wait_ge(bias1, now[0])
                    for i in range(NT):
                        last = nc.scalar.activation(h_f[:, i, :], x_t[:, i, :], ACT.Relu, bias=nb1[:, i:i + 1],
                                                    scale=rs1[:, i:i + 1])
                    last.then_inc(h_full, 1)
                if stage_d:
                    keep_ht(3, 4, now[2])
                if stage_c:
                    chunk(0, 2)
                if stage_d:
                    act.wait_ge(wh2_psum, now[2])
                    nc.scalar.activation(wh2[:, :, :], bank[:, 0:2, 0:W2N], ACT.Copy).then_inc(wh2_sb, 1)
                if stage_c:
                    chunk(1, 6)
                    slope(0)
                if stage_d:
                    slope(LAST)
                    probs(LAST)
                if stage_c:
                    chunk(2, 0)
                    probs(0)
                    slope(1)
                if stage_b:
                    act.wait_ge(sums_psum, now[0])
                    nc.scalar.activation(g_s[0][:, :, :], bank[:, 6:8, :], ACT.Copy).then_inc(g_hi, 1)
                if stage_d:
                    keep_pt(LAST, 3)
                if stage_c:
                    keep_pt(0, 2)
                    probs(1)
                    slope(2)
                if stage_d:
                    elu_exp(LAST, 0)
                if stage_c:
                    probs(2)
                    elu_exp(0, 1)
                    slope(3)
                    keep_pt(1, 5)
                    probs(3)
                if stage_d:
                    act.wait_ge(ot_psum, now[2])
                    nc.scalar.activation(ot_s[0][:, :, :], tiles(3), ACT.Copy).then_inc(ot_hi, 1)
                if stage_b:
                    act.wait_ge(h2t_psum, now[1])
                    act.wait_ge(bias2, now[0])
                    for i in range(NT):
                        last = nc.scalar.activation(h2[:, i, :], x1a[:, i, :], ACT.Relu, bias=nb2[:, i:i + 1],
                                                    scale=rs2[:, i:i + 1])
                    last.then_inc(h2_ready, 1)
                if stage_c:
                    elu_exp(1, 2)
                if stage_d:
                    act.wait_ge(rows_in, 7 * 16)
                    act.wait_ge(f_lo, now[3])
                    act.wait_ge(f_psum, now[2])
                    for i in range(DT):
                        last = nc.scalar.activation(ff[:, i, :], tiles(6)[:, i, :], ACT.Relu, bias=b1_c[:, i:i + 1])
                    last.then_inc(f_full, 1)
                if stage_c:
                    keep_pt(2, 7)
                    keep_ht(0, 3, now[1])
                    elu_exp(2, 0)
                    keep_pt(3, 6)
                    keep_ht(1, 1, now[1])
                if stage_b:
                    act.wait_ge(h2t_psum, now[0])
                    nc.scalar.activation(h2t_s[0][:, :, :], tiles(4), ACT.Copy).then_inc(h2t_hi, 1)
                if stage_d:
                    act.wait_ge(yg_ready, now[3])
                    act.wait_ge(bias3, now[2])
                    for i in range(NT):
                        last = nc.scalar.activation(yn[:, i, :], y[:, i, :], ACT.Identity, bias=nb3[:, i:i + 1],
                                                    scale=rs3[:, i:i + 1])
                    last.then_inc(yn_ready, 1)
                if stage_c:
                    keep_ht(2, 2, now[1])
                    elu_exp(3, 7)

            turns(act, turn)

        @block.vector
        def _(dve):
            dve.wait_ge(adj_in, 16)
            nc.vector.tensor_copy(adj_f[:, :, :], adj_i[:, :, :]).then_inc(adj_cast, 1)
            dve.wait_ge(adj_cast, 1)
            nc.vector.tensor_reduce(deg[:, :], adj_f[:, :, :], AX.X, ALU.add).then_inc(deg_ready, 1)
            nc.vector.tensor_scalar(mask[:, :, :], adj_f[:, :, :], 0.0, MASKED, ALU.is_le, ALU.mult).then_inc(mask_ready, 1)
            dve.wait_ge(ident_ready, 1)
            dve.wait_ge(deg_ready, 1)
            for i, c in ((0, 0), (1, 640)):
                nc.vector.tensor_scalar(ad[:, c:c + P], ident[:, :], deg[:, i:i + 1], None, ALU.mult).then_inc(diag_ready, 1)
            dve.wait_ge(adt_psum, 1)
            nc.vector.tensor_copy(ad[:, 128:640], bank[:, 0, :]).then_inc(adt_ready, 1)
            dve.wait_ge(diag_ready, 2)
            dve.wait_ge(adt_ready, 1)
            nc.vector.tensor_copy(ad_s[0][:, :], ad[:, :]).then_inc(ad_hi_ready, 1)
            dve.wait_ge(ad_hi_ready, 1)
            nc.vector.tensor_tensor(ad_s[1][:, :], ad[:, :], ad_s[0][:, :].bitcast(F32), ALU.subtract).then_inc(ad_ready, 1)
            dve.wait_ge(l0_in, 2 * 16)
            for i in range(NT):
                nc.vector.tensor_scalar(deg_b[:, i, :], b_l0[:, :], deg[:, i:i + 1], None, ALU.mult).then_inc(deg_b_ready, 1)
            dve.wait_ge(wt_psum, 1)
            wt = bank[:, 1:3, :].rearrange("p k (t n) -> p (k t) n", t=2)
            nc.vector.tensor_copy(wij_s[0][:, :, :], wt).then_inc(wij_hi_ready, 1)
            dve.wait_ge(wij_hi_ready, 1)
            nc.vector.tensor_tensor(wij_s[1][:, :, :], wt, wij_s[0][:, :, :].bitcast(F32), ALU.subtract).then_inc(wij_ready, 1)

            def halves(full, s, hi_ready, ready, n):
                nc.vector.tensor_copy(s[0][:, :, :], full[:, :, :]).then_inc(hi_ready, 1)
                dve.wait_ge(hi_ready, n)
                nc.vector.tensor_tensor(s[1][:, :, :], full[:, :, :], s[0][:, :, :].bitcast(F32),
                                        ALU.subtract).then_inc(ready, 1)

            dve.wait_ge(heads_in, 16 * (H + 1))
            for n, (h, f, s) in enumerate((h, f, s) for h in range(H) for f in range(DT) for s in range(2)):
                dve.wait_ge(wv_full, max(0, n - 1))
                nc.vector.tensor_tensor_reduce(
                    junk[:, n % 2, :], wv[:, f, NF + h * D:NF + (h + 1) * D], a_h[:, h, s * D:(s + 1) * D],
                    1.0, 0.0, ALU.mult, ALU.add, wv[:, f, s * H + h:s * H + h + 1]).then_inc(wv_full, 1)
            dve.wait_ge(wv_full, 2 * H * DT)
            halves(wv, wv_s, wv_hi_ready, wv_ready, 1)

            def setup_layer2():
                dve.wait_ge(out_in, 2 * 16)
                for n, (k, s) in enumerate((k, s) for k in range(KT) for s in range(2)):
                    dve.wait_ge(wo_full, max(0, n - 1))
                    nc.vector.tensor_tensor_reduce(
                        junk[:, n % 2, :], wo[:, k, 0:D], a_o[:, s * D:(s + 1) * D], 1.0, 0.0,
                        ALU.mult, ALU.add, wo[:, k, D + s:D + s + 1]).then_inc(wo_full, 1)
                dve.wait_ge(wo_full, 2 * KT)
                halves(wo, wo_s, wo_hi_ready, wo_ready, 1)
                dve.wait_ge(ffn_in, 2 * 16)
                halves(w1_f, w1_s, ffn_hi_ready, ffn_ready, 1)
                halves(w2_f, w2_s, ffn_hi_ready, ffn_ready, 2)

            def turn(t, stage_b, stage_c, stage_d):
                now = counts(dve, t)
                lag = [1] * H + [2]

                def statistics(src, st, mv, ve, stats, moments, var, n):
                    for i in range(NT):
                        last = nc.vector.bn_stats(st[:, i, :], src[:, i, :])
                    last.then_inc(stats, 1)
                    dve.wait_ge(deg_ready, 1)
                    dve.wait_ge(stats, n)
                    for i in range(NT):
                        last = nc.vector.bn_aggr(mv[:, i, :], st[:, i, :])
                    last.then_inc(moments, 1)
                    dve.wait_ge(moments, n)
                    nc.vector.tensor_scalar(ve[:, :], mv[:, :, 1], EPS, None, ALU.add).then_inc(var, 1)

                def shift(nb, mv, rs, rstd, bias, n):
                    dve.wait_ge(rstd, n)
                    nc.vector.scalar_tensor_tensor(out=nb[:, :], in0=mv[:, :, 0], scalar=-1.0, in1=rs[:, :],
                                                   op0=ALU.mult, op1=ALU.mult).then_inc(bias, 1)

                def keep_low(dst, src, hi, hi_done, lo_done, n):
                    dve.wait_ge(hi_done, n)
                    nc.vector.tensor_tensor(dst, src, hi.bitcast(F32), ALU.subtract).then_inc(lo_done, 1)

                def masked(h, k, col):
                    mx = m24 if h == LAST else m2
                    for i in range(NT):
                        last = nc.vector.tensor_tensor_reduce(
                            z[h][:, i, :], tiles(k)[:, h % 2, :], mask[:, i, :], 1.0, -3e38, ALU.add, ALU.max,
                            mx[:, i, col:col + 1])
                    return last

                def maxima(f1, mx, ns, nm, ns_ready, nm_ready, n):
                    nc.vector.scalar_tensor_tensor(out=ns[:, :, :], in0=mx[:, :, :], scalar=-1.0, in1=f1,
                                                   op0=ALU.mult, op1=ALU.subtract).then_inc(ns_ready, 1)
                    dve.wait_ge(ns_ready, n)
                    nc.vector.scalar_tensor_tensor(out=nm[:, :, :], in0=ns[:, :, :], scalar=SLOPE, in1=ns[:, :, :],
                                                   op0=ALU.mult, op1=ALU.min).then_inc(nm_ready, 1)

                def leaky(h):
                    dve.wait_ge(lw_ready[h], now[lag[h]])
                    for i in range(NT):
                        f1 = wh2[:, i, D:D + 1] if h == LAST else whv[:, i, h:h + 1]
                        last = nc.vector.scalar_tensor_tensor(out=lw[h][:, i, :], in0=z[h][:, i, :], scalar=f1,
                                                              in1=lw[h][:, i, :], op0=ALU.add, op1=ALU.max)
                    last.then_inc(le_ready[h], 1)

                def inverse(h):
                    dve.wait_ge(p_ready[h], now[lag[h]])
                    nc.vector.reciprocal(rinv[h][:, :], rsum[h][:, :]).then_inc(rinv_ready[h], 1)

                def elu(h, k):
                    dve.wait_ge(ex_ready[h], now[lag[h]])
                    nc.vector.tensor_scalar(p[h][:, :, :], p[h][:, :, :], 1.0, -1.0, ALU.min, ALU.add).then_inc(em_ready[h], 1)
                    dve.wait_ge(em_ready[h], now[lag[h]])
                    for i in range(NT):
                        last = nc.vector.scalar_tensor_tensor(out=hh[h][:, i, :], in0=tiles(k)[:, i, :],
                                                              scalar=rinv[h][:, i:i + 1], in1=p[h][:, i, :],
                                                              op0=ALU.mult, op1=ALU.max)
                    last.then_inc(hh_ready[h], 1)

                def ht_low(h, k, n):
                    keep_low(ht_s[1][:, DT * h:DT * h + DT, :], tiles(k), ht_s[0][:, DT * h:DT * h + DT, :],
                             ht_hi[h], ht_lo[h], n)

                if stage_b:
                    loaded = 16 * now[0] if isinstance(t, int) else dve.snap(now[0] * 16)
                    dve.wait_ge(x_loaded, loaded)
                    statistics(x_t, st1, mv1, ve1, stats1, moments1, var1, now[0])
                if stage_c:
                    dve.wait_ge(x1_beta, now[2])
                    nc.vector.tensor_copy(x1b[:, :, :], x1a[:, :, :]).then_inc(x1_kept, 1)
                if stage_b:
                    shift(nb1, mv1, rs1, rstd1, bias1, now[0])
                if stage_d:
                    ht_low(3, 4, now[2])
                if stage_b:
                    dve.wait_ge(sums_psum, now[1])
                    dve.wait_ge(h_full, now[0])
                    nc.vector.tensor_copy(h_s[0][:, :, :], h_f[:, :, :]).then_inc(h_hi, 1)
                if stage_c:
                    dve.wait_ge(wh_sb[0], now[1])
                    nc.vector.tensor_scalar(f1s[:, :, :], whv[:, :, 0:H], SLOPE, None, ALU.mult).then_inc(f1_scaled, 1)
                    for k in range(2):
                        dve.wait_ge(mask_ready, 1)
                        dve.wait_ge(rows_psum[k], now[1])
                        for h in (2 * k, 2 * k + 1):
                            last = masked(h, 4 + k, h)
                        last.then_inc(z_ready[k], 1)
                    dve.wait_ge(z_ready[1], now[1])
                    maxima(whv[:, :, 0:H], m2, nsum, negm, nsum_ready, negm_ready, now[1])
                if stage_d:
                    dve.wait_ge(wh2_sb, now[2])
                    nc.vector.tensor_scalar(f1s4[:, :, :], wh2[:, :, D:D + 1], SLOPE, None, ALU.mult).then_inc(f14_scaled, 1)
                    dve.wait_ge(mask_ready, 1)
                    dve.wait_ge(rows_psum[2], now[2])
                    masked(LAST, 2, 0).then_inc(z_ready[2], 1)
                    dve.wait_ge(z_ready[2], now[2])
                    maxima(wh2[:, :, D:D + 1], m24, nsum4, negm4, nsum4_ready, negm4_ready, now[2])
                    leaky(LAST)
                if stage_c:
                    leaky(0)
                if stage_d:
                    inverse(LAST)
                if stage_b:
                    keep_low(g_s[1][:, :, :], bank[:, 6:8, :], g_s[0][:, :, :], g_hi, g_lo, now[0])
                if stage_c:
                    leaky(1)
                    inverse(0)
                    leaky(2)
                if stage_d:
                    elu(LAST, 0)
                if stage_c:
                    inverse(1)
                    elu(0, 1)
                    leaky(3)
                if stage_b:
                    dve.wait_ge(x1_psum, now[0])
                    dve.wait_ge(xdb_ready, now[0])
                    dve.wait_ge(h2_ready, now[1])
                    nc.vector.tensor_tensor(x1a[:, :, :], tiles(4), xdb[:, :, :], ALU.add).then_inc(x1_ready, 1)
                    dve.wait_ge(x1_ready, now[0])
                    statistics(x1a, st2, mv2, ve2, stats2, moments2, var2, now[0])
                if stage_d:
                    keep_low(ot_s[1][:, :, :], tiles(3), ot_s[0][:, :, :], ot_hi, ot_lo, now[2])
                if stage_b:
                    shift(nb2, mv2, rs2, rstd2, bias2, now[0])
                if stage_c:
                    inverse(2)
                    inverse(3)
                    elu(1, 2)
                if stage_d:
                    dve.wait_ge(f_full, now[2])
                    nc.vector.tensor_copy(ff_s[0][:, :, :], ff[:, :, :]).then_inc(f_hi, 1)
                if stage_c:
                    ht_low(0, 3, now[1])
                    elu(2, 0)
                if stage_d:
                    dve.wait_ge(yn_ready, now[3])
                    dve.wait_ge(ob2_ready, now[2])
                    dve.wait_ge(y_psum, now[2])
                    nc.vector.tensor_tensor(y[:, :, :], tiles(5), ob2[:, :, :], ALU.add).then_inc(y_ready, 1)
                    dve.wait_ge(y_ready, now[2])
                    statistics(y, st3, mv3, ve3, stats3, moments3, var3, now[2])
                if stage_c:
                    ht_low(1, 1, now[1])
                if stage_b:
                    keep_low(h2t_s[1][:, :, :], tiles(4), h2t_s[0][:, :, :], h2t_hi, h2t_lo, now[0])
                if stage_d:
                    shift(nb3, mv3, rs3, rstd3, bias3, now[2])
                if stage_c:
                    ht_low(2, 2, now[1])
                    elu(3, 7)
                if isinstance(t, int) and t == 0:
                    setup_layer2()

            turns(dve, turn)


_INS = ['x', 'adj', 'L0_gnn_W', 'L0_gnn_b', 'L1_gnn_W_heads', 'L1_gnn_a_heads', 'L1_gnn_W_out', 'L1_gnn_a_out',
        'L1_gnn_w1', 'L1_gnn_b1', 'L1_gnn_w2', 'L1_gnn_b2', 'L1_gnn_ln_gamma', 'L1_gnn_ln_beta']


def kernel(**inputs):
    import numpy as _np
    import concourse.bacc as _bacc
    from concourse import mybir as _mybir
    from concourse.bass_utils import run_bass_kernel_spmd as _run

    nc = _bacc.Bacc("TRN2", target_bir_lowering=False, num_devices=1)
    arrays, args = {}, []
    for name in _INS:
        a = _np.ascontiguousarray(inputs[name])
        arrays[f"in_{name}_dram"] = a
        args.append(nc.dram_tensor(f"in_{name}_dram", a.shape, _mybir.dt.from_np(a.dtype), kind="ExternalInput").ap())
    shape = inputs['x'].shape
    args.append(nc.dram_tensor("out_0_dram", tuple(shape), _mybir.dt.float32, kind="ExternalOutput").ap())
    gnn_block_kernel(nc, *args)
    r = _run(nc, [arrays], core_ids=[0])
    return r.results[0]["out_0_dram"]
```

```python
import concourse.bass as bass
from concourse import mybir
from contextlib import ExitStack


def gnn_block_kernel(nc, x, adj, l0_w, l0_b, w_heads, a_heads, w_out, a_out, w1, b1, w2, b2, gamma, beta, out):
    F32 = mybir.dt.float32
    F32R = mybir.dt.float32r
    I32 = mybir.dt.int32
    ALU = mybir.AluOpType
    ACT = mybir.ActivationFunctionType
    AX = mybir.AxisListType

    P = 128
    BATCHES, N, D = x.shape
    H = w_heads.shape[0]
    NT = N // P
    DT = D // P
    LAST = H
    NF = 2 * H
    WVN = NF + H * D
    CHUNKS = 3
    CW = WVN // CHUNKS
    W2N = D + 2
    KT = H * DT
    LAGS = 3
    MASKED = -1e11
    SLOPE = 0.01
    EPS = 1e-5
    assert CHUNKS * CW == WVN and CW <= 512 and NT == 2 and DT == 2 and NT * D == 512

    with ExitStack() as ctx:
        def sb(name, shape, dt=F32):
            return ctx.enter_context(nc.sbuf_tensor(name, shape, dt))

        def sem(name):
            return ctx.enter_context(nc.semaphore(name))

        def split(name, shape):
            return sb(name + "_hi", shape, F32R), sb(name + "_lo", shape, F32R)

        ident = sb("ident", [P, P])
        neg_half = sb("neg_half", [P, NT])
        adj_i = sb("adj_i", [P, NT, N], I32)
        adj_f = sb("adj_f", [P, NT, N])
        deg = sb("deg", [P, NT])
        mask = sb("mask", [P, NT, N])
        ad = sb("ad", [P, 768])
        ad_s = split("ad", [P, 768])
        w_l0 = sb("w_l0", [P, DT, 2 * D])
        wij_s = split("wij", [P, 2 * DT, D])
        b_l0 = sb("b_l0", [P, D])
        deg_b = sb("deg_b", [P, NT, D])
        wv_s = split("wv", [P, DT, WVN])
        wo_s = split("wo", [P, KT, W2N])
        w1_s = split("w1", [P, DT, D])
        w2_s = split("w2", [P, DT, D])
        b1_c = sb("b1_c", [P, DT])
        b2_r = sb("b2_r", [P, NT, D])
        gamma_r = sb("gamma_r", [P, NT, D])
        beta_r = sb("beta_r", [P, NT, D])
        junk = sb("junk", [P, 2, D])

        x_t = sb("x_t", [P, NT, D])
        xdb = sb("xdb", [P, NT, D])
        st1, st2, st3 = (sb(f"st{i}", [P, NT, 6]) for i in (1, 2, 3))
        mv1, mv2, mv3 = (sb(f"mv{i}", [P, NT, 2]) for i in (1, 2, 3))
        ve1, ve2, ve3 = (sb(f"ve{i}", [P, NT]) for i in (1, 2, 3))
        rs1, rs2, rs3 = (sb(f"rs{i}", [P, NT]) for i in (1, 2, 3))
        nb1, nb2, nb3 = (sb(f"nb{i}", [P, NT]) for i in (1, 2, 3))
        h_f = sb("h_f", [P, NT, D])
        h_s = split("h", [P, NT, D])
        g_s = split("g", [P, DT, 512])
        x1a = sb("x1a", [P, NT, D])
        x1b = sb("x1b", [P, NT, D])
        x1c = sb("x1c", [P, NT, D])
        h2 = sb("h2", [P, NT, D])
        h2t_s = split("h2t", [P, DT, N])

        whv = sb("whv", [P, NT, WVN])
        wh2 = sb("wh2", [P, NT, W2N])
        f1s = sb("f1s", [P, NT, H])
        f1s4 = sb("f1s4", [P, NT, 1])
        m2 = sb("m2", [P, NT, H])
        m24 = sb("m24", [P, NT, 1])
        nsum = sb("nsum", [P, NT, H])
        nsum4 = sb("nsum4", [P, NT, 1])
        negm = sb("negm", [P, NT, H])
        negm4 = sb("negm4", [P, NT, 1])
        z = [sb(f"z{h}", [P, NT, N]) for h in range(H + 1)]
        lw = [sb(f"lw{h}", [P, NT, N]) for h in range(H + 1)]
        p = [sb(f"p{h}", [P, NT, N]) for h in range(H + 1)]
        rsum = [sb(f"rsum{h}", [P, NT]) for h in range(H + 1)]
        rinv = [sb(f"rinv{h}", [P, NT]) for h in range(H + 1)]
        pt_all = sb("pt_all", [P, H + 1, NT * N])
        hh_all = sb("hh_all", [P, H + 1, NT * D])
        pt = [pt_all[:, h, :].rearrange("p (t n) -> p t n", t=NT) for h in range(H + 1)]
        hh = [hh_all[:, h, :].rearrange("p (t n) -> p t n", t=NT) for h in range(H + 1)]
        wv = whv
        wo = pt_all[:, :, :].rearrange("p h n -> p (h n)")[:, 0:KT * W2N].rearrange("p (k n) -> p k n", k=KT)
        a_h = hh_all[:, 0:H, :]
        w1_f, w2_f = z[0], z[1]
        a_o = z[2][:, :, :].rearrange("p t n -> p (t n)")
        ht_s = split("ht", [P, KT, N])
        ot_s = split("ot", [P, DT, N])
        ob2 = sb("ob2", [P, NT, D])
        ff = sb("ff", [P, DT, N])
        ff_s = split("ff", [P, DT, N])
        y = sb("y", [P, NT, D])
        yn = sb("yn", [P, NT, D])
        yg = sb("yg", [P, NT, D])
        o_t = sb("o_t", [P, NT, D])

        bank = ctx.enter_context(nc.psum_tensor("bank", [P, 8, 512], F32))

        def tiles(k):
            return bank[:, k, :].rearrange("p (t n) -> p t n", t=2)

        adj_in, l0_in, heads_in, out_in, ffn_in, rows_in = (
            sem(n) for n in ("adj_in", "l0_in", "heads_in", "out_in", "ffn_in", "rows_in"))
        ident_zero, ident_ready, half_ready = sem("ident_zero"), sem("ident_ready"), sem("half_ready")
        adj_cast, deg_ready, mask_ready, adt_psum, adt_ready, diag_ready, ad_hi_ready, ad_ready = (
            sem(n) for n in ("adj_cast", "deg_ready", "mask_ready", "adt_psum", "adt_ready", "diag_ready",
                             "ad_hi_ready", "ad_ready"))
        wt_psum, wij_hi_ready, wij_ready, deg_b_ready = (
            sem(n) for n in ("wt_psum", "wij_hi_ready", "wij_ready", "deg_b_ready"))
        wv_full, wv_hi_ready, wv_ready, wo_full, wo_hi_ready, wo_ready, ffn_hi_ready, ffn_ready = (
            sem(n) for n in ("wv_full", "wv_hi_ready", "wv_ready", "wo_full", "wo_hi_ready", "wo_ready",
                             "ffn_hi_ready", "ffn_ready"))
        x_loaded, xdb_ready = sem("x_loaded"), sem("xdb_ready")
        stats1, moments1, var1, rstd1, bias1 = (sem(n + "1") for n in ("stats", "moments", "var", "rstd", "bias"))
        stats2, moments2, var2, rstd2, bias2 = (sem(n + "2") for n in ("stats", "moments", "var", "rstd", "bias"))
        stats3, moments3, var3, rstd3, bias3 = (sem(n + "3") for n in ("stats", "moments", "var", "rstd", "bias"))
        h_full, h_hi, h_lo, sums_psum, g_hi, g_lo = (
            sem(n) for n in ("h_full", "h_hi_done", "h_lo_done", "sums_psum", "g_hi_done", "g_lo_done"))
        x1_psum, x1_ready, x1_kept, x1_beta, h2_ready, h2t_psum, h2t_hi, h2t_lo = (
            sem(n) for n in ("x1_psum", "x1_ready", "x1_kept", "x1_beta", "h2_ready", "h2t_psum",
                             "h2t_hi_done", "h2t_lo_done"))
        wh_psum = [sem(f"wh_psum{c}") for c in range(CHUNKS)]
        wh_sb = [sem(f"wh_sb{c}") for c in range(CHUNKS)]
        wh2_psum, wh2_sb, f1_scaled, f14_scaled = (sem(n) for n in ("wh2_psum", "wh2_sb", "f1_scaled", "f14_scaled"))
        rows_psum = [sem(f"rows_psum{k}") for k in range(3)]
        z_ready = [sem(f"z_ready{k}") for k in range(3)]
        nsum_ready, nsum4_ready, negm_ready, negm4_ready = (
            sem(n) for n in ("nsum_ready", "nsum4_ready", "negm_ready", "negm4_ready"))
        per_head = ("lw_ready", "le_ready", "p_ready", "pt_psum", "pt_ready", "pv_psum", "ex_ready", "rinv_ready",
                    "em_ready", "hh_ready")
        (lw_ready, le_ready, p_ready, pt_psum, pt_ready, pv_psum, ex_ready, rinv_ready, em_ready, hh_ready) = (
            [sem(f"{n}{h}") for h in range(H + 1)] for n in per_head)
        pn_ready, ht_hi, ht_lo = ([sem(f"{n}{h}") for h in range(H)] for n in ("pn_ready", "ht_hi_done", "ht_lo_done"))
        ot_psum, ot_hi, ot_lo, ob2_ready, f_psum, f_full, f_hi, f_lo, y_psum, y_ready, yn_ready, yg_ready = (
            sem(n) for n in ("ot_psum", "ot_hi_done", "ot_lo_done", "ob2_ready", "f_psum", "f_full", "f_hi_done",
                             "f_lo_done", "y_psum", "y_ready", "yn_ready", "yg_ready"))
        out_ready, out_stored = sem("out_ready"), sem("out_stored")

        def counts(eng, t, lags=(0, 1, 2, 3, 4)):
            if isinstance(t, int):
                return {k: max(0, min(BATCHES, t + 1 - k)) for k in lags}
            return {k: eng.snap(t + 1 - k) for k in lags}

        def turns(eng, turn):
            for t in range(LAGS + 1):
                turn(t, *(k <= t for k in range(LAGS + 1)))
            with eng.Fori(LAGS + 1, BATCHES) as t:
                turn(t, *(True for k in range(LAGS + 1)))
            for t in range(BATCHES, BATCHES + LAGS):
                turn(t, *(t - k < BATCHES for k in range(LAGS + 1)))

        block = ctx.enter_context(nc.Block())

        @block.sync
        def _(sp):
            sp.dma_start(adj_i[:, :, :], adj.rearrange("(t p) m -> p t m", p=P)).then_inc(adj_in, 16)
            sp.dma_start(w_l0[:, :, :], l0_w.rearrange("(t p) d -> p t d", p=P)).then_inc(l0_in, 16)
            sp.dma_start(b_l0[:, :], l0_b.partition_broadcast(P)).then_inc(l0_in, 16)
            sp.dma_start(x_t[:, :, :], x[0].rearrange("(t p) d -> p t d", p=P)).then_inc(x_loaded, 16)
            sp.dma_start(a_h[:, :, :], a_heads.partition_broadcast(P)).then_inc(heads_in, 16)
            for h in range(H):
                sp.dma_start(wv[:, :, NF + h * D:NF + (h + 1) * D],
                             w_heads[h].rearrange("(t p) o -> p t o", p=P)).then_inc(heads_in, 16)
            sp.dma_start(a_o[:, :], a_out.partition_broadcast(P)).then_inc(out_in, 16)
            sp.dma_start(wo[:, :, 0:D], w_out.rearrange("(t p) o -> p t o", p=P)).then_inc(out_in, 16)
            sp.dma_start(w1_f[:, :, :], w1.rearrange("(t p) o -> p t o", p=P)).then_inc(ffn_in, 16)
            sp.dma_start(w2_f[:, :, :], w2.rearrange("(t p) o -> p t o", p=P)).then_inc(ffn_in, 16)
            with nc.allow_non_contiguous_dma("one column of biases"):
                sp.dma_start(b1_c[:, :], b1.rearrange("(t p) -> p t", p=P)).then_inc(rows_in, 16)
            for row, vec in ((b2_r, b2), (gamma_r, gamma), (beta_r, beta)):
                for t in range(NT):
                    sp.dma_start(row[:, t, :], vec.partition_broadcast(P)).then_inc(rows_in, 16)

            def load(b, n):
                sp.wait_ge(xdb_ready, n)
                sp.wait_ge(h_full, n)
                sp.dma_start(x_t[:, :, :], x[b].rearrange("(t p) d -> p t d", p=P)).then_inc(x_loaded, 16)

            def store(b, n):
                sp.wait_ge(out_ready, n)
                sp.dma_start(out[b].rearrange("(t p) d -> p t d", p=P), o_t[:, :, :]).then_inc(out_stored, 16)

            load(1, 1)
            load(2, 2)
            with sp.Fori(3, BATCHES) as t:
                n_loaded, n_out = sp.snap(t + 0), sp.snap(t - 2)
                load(t, n_loaded)
                store(t - 3, n_out)
            for b in range(BATCHES - 3, BATCHES):
                store(b, b + 1)
            sp.wait_ge(out_stored, 16 * BATCHES)

        @block.gpsimd
        def _(pool):
            nc.gpsimd.memset(ident[:, :], 0.0).then_inc(ident_zero, 1)
            nc.gpsimd.memset(neg_half[:, :], -0.5).then_inc(half_ready, 1)
            pool.wait_ge(ident_zero, 1)
            nc.gpsimd.affine_select(out=ident[:, :], in_=ident[:, :], compare_op=ALU.not_equal, fill=1.0, base=0,
                                    pattern=[[-1, P]], channel_multiplier=1).then_inc(ident_ready, 1)
            pool.wait_ge(half_ready, 1)

            def turn(t, stage_b, stage_c, stage_d, stage_e):
                now = counts(pool, t)
                if stage_b:
                    pool.wait_ge(var1, now[0])
                    pool.wait_ge(bias1, now[1])
                    nc.gpsimd.tensor_tensor(rs1[:, :], ve1[:, :], neg_half[:, :], ALU.pow).then_inc(rstd1, 1)
                if stage_e:
                    pool.wait_ge(yn_ready, now[3])
                    nc.gpsimd.tensor_tensor(yg[:, :, :], yn[:, :, :], gamma_r[:, :, :], ALU.mult).then_inc(yg_ready, 1)
                    stored = 16 * now[4] if isinstance(t, int) else pool.snap(now[4] * 16)
                    pool.wait_ge(yg_ready, now[3])
                    pool.wait_ge(out_stored, stored)
                    nc.gpsimd.tensor_tensor(o_t[:, :, :], yg[:, :, :], x1c[:, :, :], ALU.add).then_inc(out_ready, 1)
                if stage_b:
                    pool.wait_ge(deg_b_ready, NT)
                    pool.wait_ge(x1_ready, now[1])
                    nc.gpsimd.tensor_tensor(xdb[:, :, :], x_t[:, :, :], deg_b[:, :, :], ALU.add).then_inc(xdb_ready, 1)
                if stage_d:
                    pool.wait_ge(rows_in, 7 * 16)
                    pool.wait_ge(out_ready, now[3])
                    pool.wait_ge(x1_kept, now[2])
                    nc.gpsimd.tensor_tensor(x1c[:, :, :], x1b[:, :, :], beta_r[:, :, :], ALU.add).then_inc(x1_beta, 1)
                if stage_b:
                    pool.wait_ge(sums_psum, now[1])
                    pool.wait_ge(h_hi, now[0])
                    nc.gpsimd.tensor_tensor(h_s[1][:, :, :], h_f[:, :, :], h_s[0][:, :, :].bitcast(F32),
                                            ALU.subtract).then_inc(h_lo, 1)
                if stage_d:
                    pool.wait_ge(y_ready, now[3])
                    pool.wait_ge(hh_ready[LAST], now[2])
                    nc.gpsimd.tensor_tensor(ob2[:, :, :], hh[LAST][:, :, :], b2_r[:, :, :], ALU.add).then_inc(ob2_ready, 1)
                if stage_b:
                    pool.wait_ge(bias2, now[1])
                    pool.wait_ge(var2, now[0])
                    nc.gpsimd.tensor_tensor(rs2[:, :], ve2[:, :], neg_half[:, :], ALU.pow).then_inc(rstd2, 1)
                if stage_d:
                    pool.wait_ge(y_psum, now[3])
                    pool.wait_ge(f_hi, now[2])
                    nc.gpsimd.tensor_tensor(ff_s[1][:, :, :], ff[:, :, :], ff_s[0][:, :, :].bitcast(F32),
                                            ALU.subtract).then_inc(f_lo, 1)
                    pool.wait_ge(yn_ready, now[3])
                    pool.wait_ge(var3, now[2])
                    nc.gpsimd.tensor_tensor(rs3[:, :], ve3[:, :], neg_half[:, :], ALU.pow).then_inc(rstd3, 1)

            turns(pool, turn)

        @block.tensor
        def _(pe):
            def product(dst, terms):
                passes = [(l[i], r[j]) for l, r in terms
                          for i, j in ([(0, 0)] if len(l) == 1 else [(0, 0), (0, 1), (1, 0)])]
                for n, (lhs, rhs) in enumerate(passes):
                    last = nc.tensor.matmul(dst, lhs, rhs, start=(n == 0), stop=(n == len(passes) - 1))
                return last

            def parts(s, *index):
                return tuple(q[index] for q in s)

            def turn_over(dst, src):
                for i in range(2):
                    for j in range(2):
                        last = nc.tensor.transpose(dst[:, j, i * P:(i + 1) * P], src[:, i, j * P:(j + 1) * P], ident[:, :])
                return last

            pe.wait_ge(ident_ready, 1)
            pe.wait_ge(adj_cast, 1)
            turn_over(tiles(0), adj_f).then_inc(adt_psum, 1)
            pe.wait_ge(l0_in, 2 * 16)
            for k in range(2):
                last = turn_over(tiles(1 + k), w_l0[:, :, k * D:(k + 1) * D])
            last.then_inc(wt_psum, 1)

            def rows(dst, f2):
                for k in range(NT):
                    last = nc.tensor.transpose(dst[:, k * P:(k + 1) * P], f2[:, k, :].to_broadcast([P, P]), ident[:, :])
                return last

            def turn(t, stage_b, stage_c, stage_d, stage_e):
                now = counts(pe, t)
                nk = KT - DT

                def layer2(i, ks):
                    for k in ks:
                        for a, b in ((0, 0), (0, 1), (1, 0)):
                            last = nc.tensor.matmul(bank[:, i, 0:W2N], ht_s[a][:, k, i * P:(i + 1) * P], wo_s[b][:, k, :],
                                                    start=(k == 0 and (a, b) == (0, 0)), stop=(k == KT - 1 and (a, b) == (1, 0)))
                    return last

                def heads(c, k):
                    for i in range(NT):
                        last = product(bank[:, k + i, 0:CW], [(parts(h2t_s, slice(None), f, slice(i * P, (i + 1) * P)),
                                                               parts(wv_s, slice(None), f, slice(c * CW, (c + 1) * CW)))
                                                              for f in range(DT)])
                    last.then_inc(wh_psum[c], 1)

                def turn_p(h, k):
                    pe.wait_ge(pn_ready[h], now[1])
                    turn_over(tiles(k), p[h]).then_inc(pt_psum[h], 1)

                def head_out(h, k):
                    pe.wait_ge(pt_ready[h], now[1])
                    for i in range(DT):
                        c = NF + h * D + i * P
                        last = product(tiles(k)[:, i, :], [((whv[:, j, c:c + P],), (pt[h][:, j, :],)) for j in range(NT)])
                    last.then_inc(pv_psum[h], 1)

                if stage_c:
                    pe.wait_ge(wv_ready, 1)
                    pe.wait_ge(f_full, now[3])
                    pe.wait_ge(h2t_lo, now[1])
                    heads(0, 2)
                if stage_d:
                    pe.wait_ge(wo_ready, 1)
                    pe.wait_ge(h2t_lo, now[1])
                    for h in range(H - 1):
                        pe.wait_ge(ht_lo[h], now[2])
                    layer2(0, range(nk))
                if stage_c:
                    pe.wait_ge(pt_ready[2], now[2])
                    pe.wait_ge(wh_sb[0], now[1])
                    for h in (0, 1):
                        last = rows(tiles(5)[:, h, :], whv[:, :, H + h:H + h + 1])
                    last.then_inc(rows_psum[0], 1)
                    pe.wait_ge(pt_ready[3], now[2])
                    for h in (2, 3):
                        last = rows(tiles(6)[:, h - 2, :], whv[:, :, H + h:H + h + 1])
                    last.then_inc(rows_psum[1], 1)
                if stage_d:
                    pe.wait_ge(hh_ready[1], now[2])
                    layer2(1, range(nk))
                    pe.wait_ge(ht_lo[3], now[2])
                    for i in range(NT):
                        last = layer2(i, range(nk, KT))
                    last.then_inc(wh2_psum, 1)
                if stage_c:
                    pe.wait_ge(wh_sb[0], now[1])
                    heads(1, 2)
                if stage_d:
                    pe.wait_ge(hh_ready[3], now[2])
                    pe.wait_ge(wh2_sb, now[2])
                    rows(tiles(4)[:, 0, :], wh2[:, :, D + 1:D + 2]).then_inc(rows_psum[2], 1)
                if stage_c:
                    pe.wait_ge(wh2_sb, now[2])
                    heads(2, 0)
                    pe.wait_ge(y_ready, now[3])
                    turn_p(0, 7)
                if stage_b:
                    pe.wait_ge(ad_ready, 1)
                    pe.wait_ge(wh_sb[1], now[1])
                    pe.wait_ge(h_lo, now[0])
                    for d in range(DT):
                        for n, (dst, cols) in enumerate(((slice(0, 384), slice(0, 384)), (slice(128, 512), slice(384, 768)))):
                            for m, (a, b) in enumerate(((0, 0), (0, 1), (1, 0))):
                                last = nc.tensor.matmul(bank[:, 2 + d, dst], h_s[a][:, n, d * P:(d + 1) * P],
                                                        ad_s[b][:, cols], start=(n == 0 and m == 0),
                                                        stop=(n == 1 and m == 2), skip_group_check=True)
                    last.then_inc(sums_psum, 1)
                if stage_c:
                    pe.wait_ge(z_ready[2], now[2])
                    turn_p(1, 4)
                if stage_d:
                    pe.wait_ge(z_ready[1], now[1])
                    pe.wait_ge(p_ready[LAST], now[2])
                    turn_over(tiles(6), p[LAST]).then_inc(pt_psum[LAST], 1)
                if stage_c:
                    pe.wait_ge(z_ready[0], now[1])
                    head_out(0, 5)
                if stage_d:
                    pe.wait_ge(pt_ready[0], now[1])
                    pe.wait_ge(pt_ready[LAST], now[2])
                    for i in range(NT):
                        last = product(tiles(7)[:, i, :], [((pt[LAST][:, j, i * P:(i + 1) * P],), (wh2[:, j, 0:D],))
                                                           for j in range(NT)])
                    last.then_inc(pv_psum[LAST], 1)
                if stage_b:
                    pe.wait_ge(wij_ready, 1)
                    pe.wait_ge(wh_sb[2], now[1])
                    pe.wait_ge(g_lo, now[0])
                    for i, (d0, a0) in enumerate(((0, 128), (384, 256))):
                        last = product(tiles(0)[:, i, :],
                                       [(parts(g_s, slice(None), f, slice(c0, c0 + P)),
                                         parts(wij_s, slice(None), s * DT + f, slice(None)))
                                        for s, c0 in enumerate((d0, a0)) for f in range(DT)])
                    last.then_inc(x1_psum, 1)
                if stage_d:
                    pe.wait_ge(pt_ready[LAST], now[2])
                    pe.wait_ge(hh_ready[LAST], now[2])
                    turn_over(tiles(6), hh[LAST]).then_inc(ot_psum, 1)
                if stage_c:
                    pe.wait_ge(hh_ready[0], now[1])
                    turn_p(2, 5)
                    pe.wait_ge(wh_sb[2], now[1])
                    head_out(1, 1)
                if stage_d:
                    pe.wait_ge(ffn_ready, 2)
                    pe.wait_ge(g_lo, now[0])
                    pe.wait_ge(ot_lo, now[2])
                    for i in range(DT):
                        last = product(tiles(2)[:, i, :], [(parts(w1_s, slice(None), f, slice(i * P, (i + 1) * P)),
                                                            parts(ot_s, slice(None), f, slice(None))) for f in range(DT)])
                    last.then_inc(f_psum, 1)
                if stage_c:
                    pe.wait_ge(pt_ready[1], now[1])
                    head_out(2, 4)
                if stage_b:
                    pe.wait_ge(x1_ready, now[0])
                    pe.wait_ge(h2_ready, now[0])
                    turn_over(tiles(0), h2).then_inc(h2t_psum, 1)
                if stage_c:
                    pe.wait_ge(ot_lo, now[2])
                    turn_p(3, 6)
                if stage_d:
                    pe.wait_ge(hh_ready[LAST], now[2])
                    pe.wait_ge(f_lo, now[2])
                    for i in range(NT):
                        last = product(tiles(7)[:, i, :], [(parts(ff_s, slice(None), f, slice(i * P, (i + 1) * P)),
                                                            parts(w2_s, slice(None), f, slice(None))) for f in range(DT)])
                    last.then_inc(y_psum, 1)
                if stage_c:
                    pe.wait_ge(hh_ready[2], now[1])
                    head_out(3, 4)

            turns(pe, turn)

        @block.scalar
        def _(act):
            def turn(t, stage_b, stage_c, stage_d, stage_e):
                now = counts(act, t)
                lag = [1] * H + [2]

                def chunk(c, k):
                    act.wait_ge(wh_psum[c], now[1])
                    nc.scalar.activation(whv[:, :, c * CW:(c + 1) * CW], bank[:, k:k + 2, 0:CW],
                                         ACT.Copy).then_inc(wh_sb[c], 1)

                def slope(h):
                    if h == LAST:
                        act.wait_ge(f14_scaled, now[2])
                        act.wait_ge(z_ready[2], now[2])
                    else:
                        act.wait_ge(f1_scaled, now[1])
                        act.wait_ge(z_ready[h // 2], now[1])
                    for i in range(NT):
                        f = f1s4[:, i, 0:1] if h == LAST else f1s[:, i, h:h + 1]
                        last = nc.scalar.activation(lw[h][:, i, :], z[h][:, i, :], ACT.Identity, bias=f, scale=SLOPE)
                    last.then_inc(lw_ready[h], 1)

                def probs(h):
                    act.wait_ge(negm4_ready if h == LAST else negm_ready, now[lag[h]])
                    act.wait_ge(hh_ready[h], now[lag[h] + 1])
                    act.wait_ge(rinv_ready[h], now[lag[h] + 1])
                    act.wait_ge(le_ready[h], now[lag[h]])
                    for i in range(NT):
                        m = negm4[:, i, 0:1] if h == LAST else negm[:, i, h:h + 1]
                        last = nc.scalar.activation(p[h][:, i, :], lw[h][:, i, :], ACT.Exp, bias=m,
                                                    accum_out=rsum[h][:, i:i + 1])
                    last.then_inc(p_ready[h], 1)

                def keep_pt(h, k):
                    act.wait_ge(pt_psum[h], now[lag[h]])
                    nc.scalar.activation(pt[h][:, :, :], tiles(k), ACT.Copy).then_inc(pt_ready[h], 1)

                def elu_exp(h, k):
                    act.wait_ge(pv_psum[h], now[lag[h]])
                    if h == LAST:
                        act.wait_ge(rinv_ready[h], now[2])
                        for i in range(NT):
                            last = nc.scalar.activation(p[h][:, i, :], tiles(k)[:, i, :], ACT.Exp, scale=rinv[h][:, i:i + 1])
                    else:
                        last = nc.scalar.activation(p[h][:, :, :], tiles(k), ACT.Exp)
                    last.then_inc(ex_ready[h], 1)

                def keep_ht(h, n, n_last):
                    act.wait_ge(wh2_psum, n_last)
                    act.wait_ge(hh_ready[h], n)
                    nc.scalar.activation(ht_s[0][:, DT * h:DT * h + DT, :], hh[h][:, :, :], ACT.Copy).then_inc(ht_hi[h], 1)

                if stage_c:
                    chunk(0, 2)
                if stage_d:
                    keep_ht(3, now[2], now[3])
                if stage_b:
                    act.wait_ge(h_lo, now[1])
                    act.wait_ge(bias1, now[0])
                    for i in range(NT):
                        last = nc.scalar.activation(h_f[:, i, :], x_t[:, i, :], ACT.Relu, bias=nb1[:, i:i + 1],
                                                    scale=rs1[:, i:i + 1])
                    last.then_inc(h_full, 1)
                if stage_e:
                    act.wait_ge(yg_ready, now[4])
                    act.wait_ge(bias3, now[3])
                    for i in range(NT):
                        last = nc.scalar.activation(yn[:, i, :], y[:, i, :], ACT.Identity, bias=nb3[:, i:i + 1],
                                                    scale=rs3[:, i:i + 1])
                    last.then_inc(yn_ready, 1)
                if stage_c:
                    slope(0)
                    slope(1)
                if stage_d:
                    act.wait_ge(wh2_psum, now[2])
                    nc.scalar.activation(wh2[:, :, :], bank[:, 0:2, 0:W2N], ACT.Copy).then_inc(wh2_sb, 1)
                if stage_c:
                    probs(0)
                    chunk(1, 2)
                    probs(1)
                if stage_d:
                    slope(LAST)
                if stage_c:
                    chunk(2, 0)
                if stage_d:
                    probs(LAST)
                if stage_c:
                    keep_pt(0, 7)
                    slope(2)
                if stage_b:
                    act.wait_ge(sums_psum, now[0])
                    nc.scalar.activation(g_s[0][:, :, :], bank[:, 2:4, :], ACT.Copy).then_inc(g_hi, 1)
                if stage_c:
                    keep_pt(1, 4)
                if stage_d:
                    keep_pt(LAST, 6)
                if stage_c:
                    probs(2)
                    elu_exp(0, 5)
                    slope(3)
                if stage_d:
                    elu_exp(LAST, 7)
                if stage_c:
                    keep_ht(0, now[1], now[2])
                    probs(3)
                if stage_d:
                    act.wait_ge(ot_psum, now[2])
                    nc.scalar.activation(ot_s[0][:, :, :], tiles(6), ACT.Copy).then_inc(ot_hi, 1)
                if stage_c:
                    keep_pt(2, 5)
                    elu_exp(1, 1)
                if stage_b:
                    act.wait_ge(h2t_psum, now[1])
                    act.wait_ge(bias2, now[0])
                    for i in range(NT):
                        last = nc.scalar.activation(h2[:, i, :], x1a[:, i, :], ACT.Relu, bias=nb2[:, i:i + 1],
                                                    scale=rs2[:, i:i + 1])
                    last.then_inc(h2_ready, 1)
                if stage_d:
                    act.wait_ge(rows_in, 7 * 16)
                    act.wait_ge(f_lo, now[3])
                    act.wait_ge(f_psum, now[2])
                    for i in range(DT):
                        last = nc.scalar.activation(ff[:, i, :], tiles(2)[:, i, :], ACT.Relu, bias=b1_c[:, i:i + 1])
                    last.then_inc(f_full, 1)
                if stage_c:
                    keep_ht(1, now[1], now[2])
                    elu_exp(2, 4)
                if stage_b:
                    act.wait_ge(h2t_psum, now[0])
                    nc.scalar.activation(h2t_s[0][:, :, :], tiles(0), ACT.Copy).then_inc(h2t_hi, 1)
                if stage_c:
                    keep_pt(3, 6)
                    keep_ht(2, now[1], now[2])
                    elu_exp(3, 4)

            turns(act, turn)

        @block.vector
        def _(dve):
            dve.wait_ge(adj_in, 16)
            nc.vector.tensor_copy(adj_f[:, :, :], adj_i[:, :, :]).then_inc(adj_cast, 1)
            dve.wait_ge(adj_cast, 1)
            nc.vector.tensor_reduce(deg[:, :], adj_f[:, :, :], AX.X, ALU.add).then_inc(deg_ready, 1)
            nc.vector.tensor_scalar(mask[:, :, :], adj_f[:, :, :], 0.0, MASKED, ALU.is_le, ALU.mult).then_inc(mask_ready, 1)
            dve.wait_ge(ident_ready, 1)
            dve.wait_ge(deg_ready, 1)
            for i, c in ((0, 0), (1, 640)):
                nc.vector.tensor_scalar(ad[:, c:c + P], ident[:, :], deg[:, i:i + 1], None, ALU.mult).then_inc(diag_ready, 1)
            dve.wait_ge(adt_psum, 1)
            nc.vector.tensor_copy(ad[:, 128:640], bank[:, 0, :]).then_inc(adt_ready, 1)
            dve.wait_ge(diag_ready, 2)
            dve.wait_ge(adt_ready, 1)
            nc.vector.tensor_copy(ad_s[0][:, :], ad[:, :]).then_inc(ad_hi_ready, 1)
            dve.wait_ge(ad_hi_ready, 1)
            nc.vector.tensor_tensor(ad_s[1][:, :], ad[:, :], ad_s[0][:, :].bitcast(F32), ALU.subtract).then_inc(ad_ready, 1)
            dve.wait_ge(l0_in, 2 * 16)
            for i in range(NT):
                nc.vector.tensor_scalar(deg_b[:, i, :], b_l0[:, :], deg[:, i:i + 1], None, ALU.mult).then_inc(deg_b_ready, 1)
            dve.wait_ge(wt_psum, 1)
            wt = bank[:, 1:3, :].rearrange("p k (t n) -> p (k t) n", t=2)
            nc.vector.tensor_copy(wij_s[0][:, :, :], wt).then_inc(wij_hi_ready, 1)
            dve.wait_ge(wij_hi_ready, 1)
            nc.vector.tensor_tensor(wij_s[1][:, :, :], wt, wij_s[0][:, :, :].bitcast(F32), ALU.subtract).then_inc(wij_ready, 1)

            def halves(full, s, hi_ready, ready, n):
                nc.vector.tensor_copy(s[0][:, :, :], full[:, :, :]).then_inc(hi_ready, 1)
                dve.wait_ge(hi_ready, n)
                nc.vector.tensor_tensor(s[1][:, :, :], full[:, :, :], s[0][:, :, :].bitcast(F32),
                                        ALU.subtract).then_inc(ready, 1)

            dve.wait_ge(heads_in, 16 * (H + 1))
            for n, (h, f, s) in enumerate((h, f, s) for h in range(H) for f in range(DT) for s in range(2)):
                dve.wait_ge(wv_full, max(0, n - 1))
                nc.vector.tensor_tensor_reduce(
                    junk[:, n % 2, :], wv[:, f, NF + h * D:NF + (h + 1) * D], a_h[:, h, s * D:(s + 1) * D],
                    1.0, 0.0, ALU.mult, ALU.add, wv[:, f, s * H + h:s * H + h + 1]).then_inc(wv_full, 1)
            dve.wait_ge(wv_full, 2 * H * DT)
            halves(wv, wv_s, wv_hi_ready, wv_ready, 1)

            def setup_layer2():
                dve.wait_ge(out_in, 2 * 16)
                for n, (k, s) in enumerate((k, s) for k in range(KT) for s in range(2)):
                    dve.wait_ge(wo_full, max(0, n - 1))
                    nc.vector.tensor_tensor_reduce(
                        junk[:, n % 2, :], wo[:, k, 0:D], a_o[:, s * D:(s + 1) * D], 1.0, 0.0,
                        ALU.mult, ALU.add, wo[:, k, D + s:D + s + 1]).then_inc(wo_full, 1)
                dve.wait_ge(wo_full, 2 * KT)
                halves(wo, wo_s, wo_hi_ready, wo_ready, 1)
                dve.wait_ge(ffn_in, 2 * 16)
                halves(w1_f, w1_s, ffn_hi_ready, ffn_ready, 1)
                halves(w2_f, w2_s, ffn_hi_ready, ffn_ready, 2)

            def turn(t, stage_b, stage_c, stage_d, stage_e):
                now = counts(dve, t)
                lag = [1] * H + [2]

                def statistics(src, st, mv, ve, stats, moments, var, n):
                    for i in range(NT):
                        last = nc.vector.bn_stats(st[:, i, :], src[:, i, :])
                    last.then_inc(stats, 1)
                    dve.wait_ge(deg_ready, 1)
                    dve.wait_ge(stats, n)
                    for i in range(NT):
                        last = nc.vector.bn_aggr(mv[:, i, :], st[:, i, :])
                    last.then_inc(moments, 1)
                    dve.wait_ge(moments, n)
                    nc.vector.tensor_scalar(ve[:, :], mv[:, :, 1], EPS, None, ALU.add).then_inc(var, 1)

                def shift(nb, mv, rs, rstd, bias, n):
                    dve.wait_ge(rstd, n)
                    nc.vector.scalar_tensor_tensor(out=nb[:, :], in0=mv[:, :, 0], scalar=-1.0, in1=rs[:, :],
                                                   op0=ALU.mult, op1=ALU.mult).then_inc(bias, 1)

                def keep_low(dst, src, hi, hi_done, lo_done, n):
                    dve.wait_ge(hi_done, n)
                    nc.vector.tensor_tensor(dst, src, hi.bitcast(F32), ALU.subtract).then_inc(lo_done, 1)

                def masked(h, k, col):
                    mx = m24 if h == LAST else m2
                    for i in range(NT):
                        last = nc.vector.tensor_tensor_reduce(
                            z[h][:, i, :], tiles(k)[:, h % 2, :], mask[:, i, :], 1.0, -3e38, ALU.add, ALU.max,
                            mx[:, i, col:col + 1])
                    return last

                def maxima(f1, mx, ns, nm, ns_ready, nm_ready, n):
                    nc.vector.scalar_tensor_tensor(out=ns[:, :, :], in0=mx[:, :, :], scalar=-1.0, in1=f1,
                                                   op0=ALU.mult, op1=ALU.subtract).then_inc(ns_ready, 1)
                    dve.wait_ge(ns_ready, n)
                    nc.vector.scalar_tensor_tensor(out=nm[:, :, :], in0=ns[:, :, :], scalar=SLOPE, in1=ns[:, :, :],
                                                   op0=ALU.mult, op1=ALU.min).then_inc(nm_ready, 1)

                def leaky(h):
                    dve.wait_ge(lw_ready[h], now[lag[h]])
                    for i in range(NT):
                        f1 = wh2[:, i, D:D + 1] if h == LAST else whv[:, i, h:h + 1]
                        last = nc.vector.scalar_tensor_tensor(out=lw[h][:, i, :], in0=z[h][:, i, :], scalar=f1,
                                                              in1=lw[h][:, i, :], op0=ALU.add, op1=ALU.max)
                    last.then_inc(le_ready[h], 1)

                def inverse(h):
                    dve.wait_ge(p_ready[h], now[lag[h]])
                    nc.vector.reciprocal(rinv[h][:, :], rsum[h][:, :]).then_inc(rinv_ready[h], 1)

                def normalise(h):
                    inverse(h)
                    dve.wait_ge(rinv_ready[h], now[1])
                    for i in range(NT):
                        last = nc.vector.tensor_scalar(p[h][:, i, :], p[h][:, i, :], rinv[h][:, i:i + 1], None, ALU.mult)
                    last.then_inc(pn_ready[h], 1)

                def elu(h, k):
                    dve.wait_ge(ex_ready[h], now[lag[h]])
                    nc.vector.tensor_scalar(p[h][:, :, :], p[h][:, :, :], 1.0, -1.0, ALU.min, ALU.add).then_inc(em_ready[h], 1)
                    dve.wait_ge(em_ready[h], now[lag[h]])
                    if h == LAST:
                        for i in range(NT):
                            last = nc.vector.scalar_tensor_tensor(out=hh[h][:, i, :], in0=tiles(k)[:, i, :],
                                                                  scalar=rinv[h][:, i:i + 1], in1=p[h][:, i, :],
                                                                  op0=ALU.mult, op1=ALU.max)
                    else:
                        last = nc.vector.tensor_tensor(hh[h][:, :, :], tiles(k), p[h][:, :, :], ALU.max)
                    last.then_inc(hh_ready[h], 1)

                def ht_low(h, n):
                    keep_low(ht_s[1][:, DT * h:DT * h + DT, :], hh[h][:, :, :], ht_s[0][:, DT * h:DT * h + DT, :],
                             ht_hi[h], ht_lo[h], n)

                if stage_b:
                    loaded = 16 * now[0] if isinstance(t, int) else dve.snap(now[0] * 16)
                    dve.wait_ge(x_loaded, loaded)
                    statistics(x_t, st1, mv1, ve1, stats1, moments1, var1, now[0])
                if stage_e:
                    shift(nb3, mv3, rs3, rstd3, bias3, now[3])
                if stage_d:
                    ht_low(3, now[2])
                if stage_b:
                    shift(nb1, mv1, rs1, rstd1, bias1, now[0])
                if stage_c:
                    dve.wait_ge(wh_sb[0], now[1])
                    nc.vector.tensor_scalar(f1s[:, :, :], whv[:, :, 0:H], SLOPE, None, ALU.mult).then_inc(f1_scaled, 1)
                    for k in range(2):
                        dve.wait_ge(mask_ready, 1)
                        dve.wait_ge(rows_psum[k], now[1])
                        for h in (2 * k, 2 * k + 1):
                            last = masked(h, 5 + k, h)
                        last.then_inc(z_ready[k], 1)
                    dve.wait_ge(z_ready[1], now[1])
                    maxima(whv[:, :, 0:H], m2, nsum, negm, nsum_ready, negm_ready, now[1])
                    leaky(0)
                if stage_b:
                    dve.wait_ge(sums_psum, now[1])
                    dve.wait_ge(h_full, now[0])
                    nc.vector.tensor_copy(h_s[0][:, :, :], h_f[:, :, :]).then_inc(h_hi, 1)
                if stage_c:
                    leaky(1)
                if stage_d:
                    dve.wait_ge(wh2_sb, now[2])
                    nc.vector.tensor_scalar(f1s4[:, :, :], wh2[:, :, D:D + 1], SLOPE, None, ALU.mult).then_inc(f14_scaled, 1)
                    dve.wait_ge(mask_ready, 1)
                    dve.wait_ge(rows_psum[2], now[2])
                    masked(LAST, 4, 0).then_inc(z_ready[2], 1)
                    dve.wait_ge(z_ready[2], now[2])
                    maxima(wh2[:, :, D:D + 1], m24, nsum4, negm4, nsum4_ready, negm4_ready, now[2])
                if stage_c:
                    normalise(0)
                if stage_d:
                    leaky(LAST)
                if stage_c:
                    normalise(1)
                    dve.wait_ge(x1_beta, now[2])
                    nc.vector.tensor_copy(x1b[:, :, :], x1a[:, :, :]).then_inc(x1_kept, 1)
                    leaky(2)
                if stage_d:
                    inverse(LAST)
                if stage_b:
                    keep_low(g_s[1][:, :, :], bank[:, 2:4, :], g_s[0][:, :, :], g_hi, g_lo, now[0])
                if stage_c:
                    normalise(2)
                    elu(0, 5)
                    leaky(3)
                if stage_d:
                    elu(LAST, 7)
                if stage_c:
                    ht_low(0, now[1])
                if stage_b:
                    dve.wait_ge(x1_psum, now[0])
                    dve.wait_ge(xdb_ready, now[0])
                    dve.wait_ge(h2_ready, now[1])
                    nc.vector.tensor_tensor(x1a[:, :, :], tiles(0), xdb[:, :, :], ALU.add).then_inc(x1_ready, 1)
                if stage_d:
                    keep_low(ot_s[1][:, :, :], tiles(6), ot_s[0][:, :, :], ot_hi, ot_lo, now[2])
                if stage_b:
                    dve.wait_ge(x1_ready, now[0])
                    statistics(x1a, st2, mv2, ve2, stats2, moments2, var2, now[0])
                if stage_c:
                    normalise(3)
                if stage_b:
                    shift(nb2, mv2, rs2, rstd2, bias2, now[0])
                if stage_c:
                    elu(1, 1)
                if stage_d:
                    dve.wait_ge(f_full, now[2])
                    nc.vector.tensor_copy(ff_s[0][:, :, :], ff[:, :, :]).then_inc(f_hi, 1)
                if stage_c:
                    ht_low(1, now[1])
                    elu(2, 4)
                if stage_b:
                    keep_low(h2t_s[1][:, :, :], tiles(0), h2t_s[0][:, :, :], h2t_hi, h2t_lo, now[0])
                if stage_d:
                    dve.wait_ge(yn_ready, now[3])
                    dve.wait_ge(ob2_ready, now[2])
                    dve.wait_ge(y_psum, now[2])
                    nc.vector.tensor_tensor(y[:, :, :], tiles(7), ob2[:, :, :], ALU.add).then_inc(y_ready, 1)
                if stage_c:
                    ht_low(2, now[1])
                if stage_d:
                    dve.wait_ge(y_ready, now[2])
                    statistics(y, st3, mv3, ve3, stats3, moments3, var3, now[2])
                if stage_c:
                    elu(3, 4)
                if isinstance(t, int) and t == 0:
                    setup_layer2()

            turns(dve, turn)


_INS = ['x', 'adj', 'L0_gnn_W', 'L0_gnn_b', 'L1_gnn_W_heads', 'L1_gnn_a_heads', 'L1_gnn_W_out', 'L1_gnn_a_out',
        'L1_gnn_w1', 'L1_gnn_b1', 'L1_gnn_w2', 'L1_gnn_b2', 'L1_gnn_ln_gamma', 'L1_gnn_ln_beta']


def kernel(**inputs):
    import numpy as _np
    import concourse.bacc as _bacc
    from concourse import mybir as _mybir
    from concourse.bass_utils import run_bass_kernel_spmd as _run

    nc = _bacc.Bacc("TRN2", target_bir_lowering=False, num_devices=1)
    arrays, args = {}, []
    for name in _INS:
        a = _np.ascontiguousarray(inputs[name])
        arrays[f"in_{name}_dram"] = a
        args.append(nc.dram_tensor(f"in_{name}_dram", a.shape, _mybir.dt.from_np(a.dtype), kind="ExternalInput").ap())
    shape = inputs['x'].shape
    args.append(nc.dram_tensor("out_0_dram", tuple(shape), _mybir.dt.float32, kind="ExternalOutput").ap())
    gnn_block_kernel(nc, *args)
    r = _run(nc, [arrays], core_ids=[0])
    return r.results[0]["out_0_dram"]
```

```python
import concourse.bass as bass
from concourse import mybir
from contextlib import ExitStack


def gnn_block_kernel(nc, x, adj, l0_w, l0_b, w_heads, a_heads, w_out, a_out, w1, b1, w2, b2, gamma, beta, out):
    F32 = mybir.dt.float32
    F32R = mybir.dt.float32r
    I32 = mybir.dt.int32
    ALU = mybir.AluOpType
    ACT = mybir.ActivationFunctionType
    AX = mybir.AxisListType

    P = 128
    BATCHES, N, D = x.shape
    H = w_heads.shape[0]
    NT = N // P
    DT = D // P
    LAST = H
    NF = 2 * H
    WVN = NF + H * D
    CHUNKS = 3
    CW = WVN // CHUNKS
    W2N = D + 2
    KT = H * DT
    UNROLL = 2
    LAGS = 3
    MASKED = -1e11
    SLOPE = 0.01
    EPS = 1e-5
    assert (BATCHES - LAGS - 1) % UNROLL == 0 and CHUNKS * CW == WVN and CW <= 512 and NT == 2 and DT == 2 and NT * D == 512

    with ExitStack() as ctx:
        def sb(name, shape, dt=F32):
            return ctx.enter_context(nc.sbuf_tensor(name, shape, dt))

        def sem(name):
            return ctx.enter_context(nc.semaphore(name))

        def split(name, shape):
            return sb(name + "_hi", shape, F32R), sb(name + "_lo", shape, F32R)

        ident = sb("ident", [P, P])
        neg_half = sb("neg_half", [P, NT])
        adj_i = sb("adj_i", [P, NT, N], I32)
        deg = sb("deg", [P, NT])
        mask = sb("mask", [P, NT, N])
        ad_s = split("ad", [P, 768])
        wij_s = split("wij", [P, 2 * DT, D])
        b_l0 = sb("b_l0", [P, D])
        deg_b = sb("deg_b", [P, NT, D])
        wv_s = split("wv", [P, DT, WVN])
        wo_s = split("wo", [P, KT, W2N])
        w1_s = split("w1", [P, DT, D])
        w2_s = split("w2", [P, DT, D])
        b1_c = sb("b1_c", [P, DT])
        b2_r = sb("b2_r", [P, NT, D])
        gamma_r = sb("gamma_r", [P, NT, D])
        beta_r = sb("beta_r", [P, NT, D])

        x_t = sb("x_t", [P, NT, D])
        xdb = sb("xdb", [P, NT, D])
        st1, st2, st3 = (sb(f"st{i}", [P, NT, 6]) for i in (1, 2, 3))
        mv1, mv2, mv3 = (sb(f"mv{i}", [P, NT, 2]) for i in (1, 2, 3))
        ve1, ve2, ve3 = (sb(f"ve{i}", [P, NT]) for i in (1, 2, 3))
        rs1, rs2, rs3 = (sb(f"rs{i}", [P, NT]) for i in (1, 2, 3))
        nb1, nb2, nb3 = (sb(f"nb{i}", [P, NT]) for i in (1, 2, 3))
        h_f = sb("h_f", [P, NT, D])
        h_s = split("h", [P, NT, D])
        g_s = split("g", [P, DT, 512])
        x1_h2 = sb("x1_h2", [P, 2, NT * D])
        x1a, h2 = (x1_h2[:, i, :].rearrange("p (t d) -> p t d", t=NT) for i in range(2))
        x1b = sb("x1b", [P, NT, D])
        x1c = sb("x1c", [P, NT, D])
        h2t_s = split("h2t", [P, DT, N])

        f12 = sb("f12", [P, NT, NF])
        f12_2 = sb("f12_2", [P, NT, 2])
        wh_s = split("wh", [P, NT, WVN])
        w2h_s = split("w2h", [P, NT, D])
        m2 = sb("m2", [P, NT, H])
        m24 = sb("m24", [P, NT, 1])
        nsum = sb("nsum", [P, NT, H])
        nsum4 = sb("nsum4", [P, NT, 1])
        negm = sb("negm", [P, NT, H])
        negm4 = sb("negm4", [P, NT, 1])
        z_all = sb("z_all", [P, H + 1, NT * N])
        p_all = sb("p_all", [P, H + 1, NT * N])
        hh_all = sb("hh_all", [P, H + 1, NT * D])
        z, p, hh = ([a[:, h, :].rearrange("p (t n) -> p t n", t=NT) for h in range(H + 1)] for a in (z_all, p_all, hh_all))
        pt_hi = [sb(f"pt_hi{h}", [P, NT, N], F32R) for h in range(H + 1)]
        pt_lo = [sb(f"pt_lo{h}", [P, NT, N], F32R) for h in range(H + 1)]
        rsum = [sb(f"rsum{h}", [P, NT]) for h in range(H + 1)]
        rinv = [sb(f"rinv{h}", [P, NT]) for h in range(H + 1)]
        ht_s = split("ht", [P, KT, N])
        ot_s = split("ot", [P, DT, N])
        ob2 = sb("ob2", [P, NT, D])
        ff_s = split("ff", [P, DT, N])
        ff_y = sb("ff_y", [P, 2, NT * D])
        ff, y = (ff_y[:, i, :].rearrange("p (t d) -> p t d", t=NT) for i in range(2))
        yn = sb("yn", [P, NT, D])
        yg = sb("yg", [P, NT, D])
        o_t = sb("o_t", [P, NT, D])
        adj_f = o_t
        ad = ff_y[:, :, :].rearrange("p k n -> p (k n)")[:, 0:768]
        w_l0 = x1_h2
        wv = z_all[:, :, :].rearrange("p h n -> p (h n)")[:, 0:DT * WVN].rearrange("p (k n) -> p k n", k=DT)
        wo = hh_all[:, :, :].rearrange("p h n -> p (h n)")[:, 0:KT * W2N].rearrange("p (k n) -> p k n", k=KT)
        a_h = p_all[:, 0:H, :]
        w1_f, w2_f = yn, yg
        a_o = ob2[:, :, :].rearrange("p t n -> p (t n)")
        junk = p[LAST]

        bank = ctx.enter_context(nc.psum_tensor("bank", [P, 8, 512], F32))

        def tiles(k):
            return bank[:, k, :].rearrange("p (t n) -> p t n", t=2)

        bank_wh = [2, 3, 0]
        bank_rows = [4, 1, 7]
        bank_pt = [2, 7, 2, 0, 5]
        bank_pv = [4, 5, 6, 7, 7]
        BANK_L2, BANK_SUMS, BANK_X1, BANK_H2T = 0, 5, 6, 1
        BANK_OT, BANK_FF, BANK_Y = 3, 0, 6
        BANK_W, BANK_ADJ = 0, 2

        adj_in, l0_in, heads_in, late_in = (sem(n) for n in ("adj_in", "l0_in", "heads_in", "late_in"))
        constants, ident_ready = sem("constants"), sem("ident_ready")
        adj_cast, deg_ready, mask_ready, setup_psum, ad_full, ad_ready, wij_ready, deg_b_ready = (
            sem(n) for n in ("adj_cast", "deg_ready", "mask_ready", "setup_psum", "ad_full", "ad_ready", "wij_ready",
                             "deg_b_ready"))
        column_ready = sem("column_ready")
        high_ready = sem("high_ready")
        wv_ready, late_ready = sem("wv_ready"), sem("late_ready")
        x_loaded, xdb_ready = sem("x_loaded"), sem("xdb_ready")
        stats1, moments1, var1, rstd1, bias1 = (sem(n + "1") for n in ("stats", "moments", "var", "rstd", "bias"))
        stats2, moments2, var2, rstd2, bias2 = (sem(n + "2") for n in ("stats", "moments", "var", "rstd", "bias"))
        stats3, moments3, var3, rstd3, bias3 = (sem(n + "3") for n in ("stats", "moments", "var", "rstd", "bias"))
        h_full, h_hi, h_lo, sums_psum, g_hi, g_lo = (
            sem(n) for n in ("h_full", "h_hi_done", "h_lo_done", "sums_psum", "g_hi_done", "g_lo_done"))
        x1_psum, x1_ready, x1_kept, x1_beta, h2_ready, h2t_psum, h2t_hi, h2t_lo = (
            sem(n) for n in ("x1_psum", "x1_ready", "x1_kept", "x1_beta", "h2_ready", "h2t_psum",
                             "h2t_hi_done", "h2t_lo_done"))
        wh_psum, wh_hi, wh_lo = ([sem(f"{n}{c}") for c in range(CHUNKS)] for n in ("wh_psum", "wh_hi", "wh_lo"))
        l2_psum, w2_hi, w2_lo, f12_ready, f12_2_ready = (
            sem(n) for n in ("l2_psum", "w2_hi", "w2_lo", "f12_ready", "f12_2_ready"))
        rows_psum = [sem(f"rows_psum{k}") for k in range(3)]
        z_ready = [sem(f"z_ready{k}") for k in range(3)]
        nsum_ready, nsum4_ready, negm_ready, negm4_ready = (
            sem(n) for n in ("nsum_ready", "nsum4_ready", "negm_ready", "negm4_ready"))
        per_head = ("e_ready", "leaky_ready", "p_ready", "pt_psum", "pt_hi_done", "pt_lo_done", "pv_psum", "ex_ready",
                    "rinv_ready", "em_ready", "hh_ready")
        (e_ready, leaky_ready, p_ready, pt_psum, pt_hi_done, pt_lo_done, pv_psum, ex_ready, rinv_ready, em_ready,
         hh_ready) = ([sem(f"{n}{h}") for h in range(H + 1)] for n in per_head)
        pn_ready, ht_hi, ht_lo = ([sem(f"{n}{h}") for h in range(H)] for n in ("pn_ready", "ht_hi_done", "ht_lo_done"))
        ot_psum, ot_hi, ot_lo, ob2_ready, f_psum, f_full, f_hi, f_lo, y_psum, y_ready, yn_ready, yg_ready = (
            sem(n) for n in ("ot_psum", "ot_hi_done", "ot_lo_done", "ob2_ready", "f_psum", "f_full", "f_hi_done",
                             "f_lo_done", "y_psum", "y_ready", "yn_ready", "yg_ready"))
        out_ready, out_stored = sem("out_ready"), sem("out_stored")

        def counts(eng, t, lags=(0, 1, 2, 3, 4)):
            if isinstance(t, int):
                return {k: max(0, min(BATCHES, t + 1 - k)) for k in lags}
            return {k: eng.snap(t + 1 - k) for k in lags}

        def turns(eng, turn):
            for t in range(LAGS + 1):
                turn(t, *(k <= t for k in range(LAGS + 1)))
            with eng.Fori(LAGS + 1, BATCHES, UNROLL) as t:
                for k in range(UNROLL):
                    turn(t + k, *(True for _ in range(LAGS + 1)))
            for t in range(BATCHES, BATCHES + LAGS):
                turn(t, *(t - k < BATCHES for k in range(LAGS + 1)))

        block = ctx.enter_context(nc.Block())

        @block.sync
        def _(sp):
            sp.dma_start(x_t[:, :, :], x[0].rearrange("(t p) d -> p t d", p=P)).then_inc(x_loaded, 16)
            sp.dma_start(adj_i[:, :, :], adj.rearrange("(t p) m -> p t m", p=P)).then_inc(adj_in, 16)
            sp.dma_start(b_l0[:, :], l0_b.partition_broadcast(P)).then_inc(l0_in, 16)
            sp.dma_start(w_l0[:, :, :], l0_w.rearrange("(t p) d -> p t d", p=P)).then_inc(l0_in, 16)
            sp.dma_start(a_h[:, :, :], a_heads.partition_broadcast(P)).then_inc(heads_in, 16)
            for h in range(H):
                sp.dma_start(wv[:, :, NF + h * D:NF + (h + 1) * D],
                             w_heads[h].rearrange("(t p) o -> p t o", p=P)).then_inc(heads_in, 16)
            sp.dma_start(a_o[:, :], a_out.partition_broadcast(P)).then_inc(late_in, 16)
            sp.dma_start(wo[:, :, 0:D], w_out.rearrange("(t p) o -> p t o", p=P)).then_inc(late_in, 16)
            sp.dma_start(w1_f[:, :, :], w1.rearrange("(t p) o -> p t o", p=P)).then_inc(late_in, 16)
            sp.dma_start(w2_f[:, :, :], w2.rearrange("(t p) o -> p t o", p=P)).then_inc(late_in, 16)
            with nc.allow_non_contiguous_dma("one column of biases"):
                sp.dma_start(b1_c[:, :], b1.rearrange("(t p) -> p t", p=P)).then_inc(late_in, 16)
            for row, vec in ((b2_r, b2), (gamma_r, gamma), (beta_r, beta)):
                for t in range(NT):
                    sp.dma_start(row[:, t, :], vec.partition_broadcast(P)).then_inc(late_in, 16)

            def load(b, n):
                sp.wait_ge(xdb_ready, n)
                sp.wait_ge(h_full, n)
                sp.dma_start(x_t[:, :, :], x[b].rearrange("(t p) d -> p t d", p=P)).then_inc(x_loaded, 16)

            def store(b, n):
                sp.wait_ge(out_ready, n)
                sp.dma_start(out[b].rearrange("(t p) d -> p t d", p=P), o_t[:, :, :]).then_inc(out_stored, 16)

            load(1, 1)
            load(2, 2)
            with sp.Fori(3, BATCHES) as t:
                n_loaded, n_out = sp.snap(t + 0), sp.snap(t - 2)
                load(t, n_loaded)
                store(t - 3, n_out)
            for b in range(BATCHES - 3, BATCHES):
                store(b, b + 1)
            sp.wait_ge(out_stored, 16 * BATCHES)

        @block.gpsimd
        def _(pool):
            nc.gpsimd.memset(ident[:, :], 0.0).then_inc(constants, 1)
            nc.gpsimd.memset(neg_half[:, :], -0.5).then_inc(constants, 1)
            pool.wait_ge(constants, 1)
            nc.gpsimd.affine_select(out=ident[:, :], in_=ident[:, :], compare_op=ALU.not_equal, fill=1.0, base=0,
                                    pattern=[[-1, P]], channel_multiplier=1).then_inc(ident_ready, 1)
            pool.wait_ge(constants, 2)

            def weights_low(n, full, s, ready):
                pool.wait_ge(high_ready, n)
                nc.gpsimd.tensor_tensor(s[1][:, :, :], full, s[0][:, :, :].bitcast(F32), ALU.subtract).then_inc(ready, 1)

            def heads_low():
                weights_low(2, wv, wv_s, wv_ready)

            def layer2_low():
                weights_low(3, wo, wo_s, late_ready)

            def ffn_low():
                weights_low(4, w1_f[:, :, :], w1_s, late_ready)
                weights_low(5, w2_f[:, :, :], w2_s, late_ready)

            def turn(t, stage_b, stage_c, stage_d, stage_e):
                now = counts(pool, t)
                loaded = 16 * now[0] if isinstance(t, int) else pool.snap(now[0] * 16)
                stored = 16 * now[4] if isinstance(t, int) else pool.snap(now[4] * 16)

                def rstd(rs, ve, var, used, ready, n, n_last):
                    pool.wait_ge(var, n)
                    pool.wait_ge(used, n_last)
                    nc.gpsimd.tensor_tensor(rs[:, :], ve[:, :], neg_half[:, :], ALU.pow).then_inc(ready, 1)

                def times_gamma(n, n_last):
                    pool.wait_ge(out_ready, n_last)
                    pool.wait_ge(yn_ready, n)
                    nc.gpsimd.tensor_tensor(yg[:, :, :], yn[:, :, :], gamma_r[:, :, :], ALU.mult).then_inc(yg_ready, 1)

                def output(n, n_last):
                    pool.wait_ge(yg_ready, n)
                    pool.wait_ge(x1_beta, n)
                    pool.wait_ge(out_stored, stored)
                    nc.gpsimd.tensor_tensor(o_t[:, :, :], yg[:, :, :], x1c[:, :, :], ALU.add).then_inc(out_ready, 1)

                def x_plus_bias(n, n_last):
                    pool.wait_ge(deg_b_ready, NT)
                    pool.wait_ge(x_loaded, loaded)
                    pool.wait_ge(x1_ready, n_last)
                    nc.gpsimd.tensor_tensor(xdb[:, :, :], x_t[:, :, :], deg_b[:, :, :], ALU.add).then_inc(xdb_ready, 1)

                def x1_plus_beta(n, n_last):
                    pool.wait_ge(late_in, 11 * 16)
                    pool.wait_ge(out_ready, n_last)
                    pool.wait_ge(x1_kept, n)
                    nc.gpsimd.tensor_tensor(x1c[:, :, :], x1b[:, :, :], beta_r[:, :, :], ALU.add).then_inc(x1_beta, 1)

                def out_plus_b2(n, n_last):
                    pool.wait_ge(y_ready, n_last)
                    pool.wait_ge(hh_ready[LAST], n)
                    nc.gpsimd.tensor_tensor(ob2[:, :, :], hh[LAST][:, :, :], b2_r[:, :, :], ALU.add).then_inc(ob2_ready, 1)

                def ht_low(h, n):
                    pool.wait_ge(ht_hi[h], n)
                    nc.gpsimd.tensor_tensor(ht_s[1][:, DT * h:DT * h + DT, :], hh[h][:, :, :],
                                            ht_s[0][:, DT * h:DT * h + DT, :].bitcast(F32), ALU.subtract).then_inc(ht_lo[h], 1)

                def h_low(n, n_last):
                    pool.wait_ge(sums_psum, n_last)
                    pool.wait_ge(h_hi, n)
                    nc.gpsimd.tensor_tensor(h_s[1][:, :, :], h_f[:, :, :], h_s[0][:, :, :].bitcast(F32),
                                            ALU.subtract).then_inc(h_lo, 1)

                def hidden_low(n):
                    pool.wait_ge(f_hi, n)
                    nc.gpsimd.tensor_tensor(ff_s[1][:, :, :], ff[:, :, :], ff_s[0][:, :, :].bitcast(F32),
                                            ALU.subtract).then_inc(f_lo, 1)

                def pt_low(h, n):
                    pool.wait_ge(pt_hi_done[h], n)
                    nc.gpsimd.tensor_tensor(pt_lo[h][:, :, :], p[h][:, :, :], pt_hi[h][:, :, :].bitcast(F32),
                                            ALU.subtract).then_inc(pt_lo_done[h], 1)

                if stage_d:
                    ht_low(1, now[2])
                if stage_b:
                    rstd(rs1, ve1, var1, bias1, rstd1, now[0], now[1])
                if isinstance(t, int) and t == 1:
                    layer2_low()
                if stage_e:
                    hidden_low(now[3])
                if stage_d:
                    ht_low(0, now[2])
                if stage_b:
                    h_low(now[0], now[1])
                if stage_d:
                    ht_low(3, now[2])
                if stage_e:
                    rstd(rs3, ve3, var3, bias3, rstd3, now[3], now[4])
                if stage_b:
                    x_plus_bias(now[0], now[1])
                if isinstance(t, int) and t == 0:
                    heads_low()
                if stage_e:
                    times_gamma(now[3], now[4])
                    output(now[3], now[4])
                if stage_d:
                    x1_plus_beta(now[2], now[3])
                if stage_c:
                    pt_low(2, now[1])
                    pt_low(1, now[1])
                if stage_b:
                    rstd(rs2, ve2, var2, bias2, rstd2, now[0], now[1])
                if isinstance(t, int) and t == 1:
                    ffn_low()
                if stage_c:
                    pt_low(0, now[1])
                if stage_d:
                    out_plus_b2(now[2], now[3])
                if stage_c:
                    pt_low(3, now[1])
                    ht_low(2, now[1])

            turns(pool, turn)

        @block.tensor
        def _(pe):
            def product(dst, terms):
                passes = [(l[i], r[j]) for l, r in terms
                          for i, j in ([(0, 0)] if len(l) == 1 else [(0, 0), (0, 1), (1, 0)])]
                for n, (lhs, rhs) in enumerate(passes):
                    last = nc.tensor.matmul(dst, lhs, rhs, start=(n == 0), stop=(n == len(passes) - 1))
                return last

            def parts(s, *index):
                return tuple(q[index] for q in s)

            def turn_over(dst, src):
                for i in range(2):
                    for j in range(2):
                        last = nc.tensor.transpose(dst[:, j, i * P:(i + 1) * P], src[:, i, j * P:(j + 1) * P], ident[:, :])
                return last

            pe.wait_ge(ident_ready, 1)
            pe.wait_ge(adj_cast, 1)
            turn_over(tiles(BANK_ADJ), adj_f).then_inc(setup_psum, 1)
            pe.wait_ge(l0_in, 2 * 16)
            for k in range(2):
                last = turn_over(tiles(BANK_W + k), w_l0[:, :, k * D:(k + 1) * D])
            last.then_inc(setup_psum, 1)

            def rows(dst, f2):
                for k in range(NT):
                    last = nc.tensor.transpose(dst[:, k * P:(k + 1) * P], f2[:, k, :].to_broadcast([P, P]), ident[:, :])
                return last

            def turn(t, stage_b, stage_c, stage_d, stage_e):
                now = counts(pe, t)

                def features(c, n):
                    pe.wait_ge(wv_ready, 1)
                    pe.wait_ge(h2t_lo, n)
                    for i in range(NT):
                        last = product(bank[:, bank_wh[c] + i, 0:CW],
                                       [(parts(h2t_s, slice(None), f, slice(i * P, (i + 1) * P)),
                                         parts(wv_s, slice(None), f, slice(c * CW, (c + 1) * CW))) for f in range(DT)])
                    last.then_inc(wh_psum[c], 1)

                def rows_of(k, n):
                    if k == 2:
                        pe.wait_ge(f12_2_ready, n)
                        last = rows(tiles(bank_rows[k])[:, 0, :], f12_2[:, :, 1:2])
                    else:
                        pe.wait_ge(f12_ready, n)
                        for j in range(2):
                            last = rows(tiles(bank_rows[k])[:, j, :], f12[:, :, H + 2 * k + j:H + 2 * k + j + 1])
                    last.then_inc(rows_psum[k], 1)

                def layer2(i, ks):
                    for k in ks:
                        for a, b in ((0, 0), (0, 1), (1, 0)):
                            last = nc.tensor.matmul(bank[:, BANK_L2 + i, 0:W2N], ht_s[a][:, k, i * P:(i + 1) * P],
                                                    wo_s[b][:, k, :], start=(k == 0 and (a, b) == (0, 0)),
                                                    stop=(k == KT - 1 and (a, b) == (1, 0)))
                    return last

                def layer2_first(i, n):
                    if i == 0:
                        pe.wait_ge(late_ready, 1)
                        for h in range(H - 1):
                            pe.wait_ge(ht_lo[h], n)
                    layer2(i, range(KT - DT))

                def layer2_last(n):
                    pe.wait_ge(ht_lo[H - 1], n)
                    for i in range(NT):
                        last = layer2(i, range(KT - DT, KT))
                    last.then_inc(l2_psum, 1)

                def turn_p(h, n):
                    pe.wait_ge(p_ready[h] if h == LAST else pn_ready[h], n)
                    turn_over(tiles(bank_pt[h]), p[h]).then_inc(pt_psum[h], 1)

                def head_out(h, n):
                    pe.wait_ge(pt_lo_done[h], n)
                    if h == LAST:
                        pe.wait_ge(w2_lo, n)
                    else:
                        for c in range((NF + h * D) // CW, (NF + (h + 1) * D - 1) // CW + 1):
                            pe.wait_ge(wh_lo[c], n)
                    pt = (pt_hi[h], pt_lo[h])
                    for i in range(NT):
                        if h == LAST:
                            terms = [(parts(pt, slice(None), j, slice(i * P, (i + 1) * P)),
                                      parts(w2h_s, slice(None), j, slice(None))) for j in range(NT)]
                        else:
                            c = NF + h * D + i * P
                            terms = [(parts(wh_s, slice(None), j, slice(c, c + P)),
                                      parts(pt, slice(None), j, slice(None))) for j in range(NT)]
                        last = product(tiles(bank_pv[h])[:, i, :], terms)
                    last.then_inc(pv_psum[h], 1)

                def neighbour_sums(n):
                    pe.wait_ge(ad_ready, 1)
                    pe.wait_ge(h_lo, n)
                    for d in range(DT):
                        for k, (dst, cols) in enumerate(((slice(0, 384), slice(0, 384)), (slice(128, 512), slice(384, 768)))):
                            for m, (a, b) in enumerate(((0, 0), (0, 1), (1, 0))):
                                last = nc.tensor.matmul(bank[:, BANK_SUMS + d, dst], h_s[a][:, k, d * P:(d + 1) * P],
                                                        ad_s[b][:, cols], start=(k == 0 and m == 0),
                                                        stop=(k == 1 and m == 2), skip_group_check=True)
                    last.then_inc(sums_psum, 1)

                def first_products(n):
                    pe.wait_ge(wij_ready, 1)
                    pe.wait_ge(g_lo, n)
                    for i, (d0, a0) in enumerate(((0, 128), (384, 256))):
                        last = product(tiles(BANK_X1)[:, i, :],
                                       [(parts(g_s, slice(None), f, slice(c0, c0 + P)),
                                         parts(wij_s, slice(None), s * DT + f, slice(None)))
                                        for s, c0 in enumerate((d0, a0)) for f in range(DT)])
                    last.then_inc(x1_psum, 1)

                def turn_h2(n):
                    pe.wait_ge(h2_ready, n)
                    turn_over(tiles(BANK_H2T), h2).then_inc(h2t_psum, 1)

                def turn_out(n):
                    pe.wait_ge(hh_ready[LAST], n)
                    turn_over(tiles(BANK_OT), hh[LAST]).then_inc(ot_psum, 1)

                def ffn_hidden(n):
                    pe.wait_ge(late_ready, 3)
                    pe.wait_ge(ot_lo, n)
                    for i in range(DT):
                        last = product(tiles(BANK_FF)[:, i, :], [(parts(w1_s, slice(None), f, slice(i * P, (i + 1) * P)),
                                                                  parts(ot_s, slice(None), f, slice(None))) for f in range(DT)])
                    last.then_inc(f_psum, 1)

                def ffn_output(n):
                    pe.wait_ge(f_lo, n)
                    for i in range(NT):
                        last = product(tiles(BANK_Y)[:, i, :], [(parts(ff_s, slice(None), f, slice(i * P, (i + 1) * P)),
                                                                 parts(w2_s, slice(None), f, slice(None))) for f in range(DT)])
                    last.then_inc(y_psum, 1)

                if stage_c:
                    if isinstance(t, int):
                        pe.wait_ge(pt_hi_done[2], now[2])
                        pe.wait_ge(wh_lo[1], now[2])
                    pe.wait_ge(pt_hi_done[0], now[2])
                    pe.wait_ge(ot_lo, now[3])
                    features(0, now[1])
                    if isinstance(t, int):
                        pe.wait_ge(wh_lo[1], now[2])
                    pe.wait_ge(hh_ready[0], now[2])
                    rows_of(0, now[1])
                    if isinstance(t, int):
                        pe.wait_ge(wh_lo[2], now[2])
                        pe.wait_ge(w2_lo, now[3])
                    pe.wait_ge(h2t_lo, now[1])
                    rows_of(1, now[1])
                if stage_e:
                    if isinstance(t, int):
                        pe.wait_ge(x1_ready, now[1])
                        pe.wait_ge(g_lo, now[1])
                    pe.wait_ge(hh_ready[2], now[2])
                    ffn_output(now[3])
                if stage_d:
                    if isinstance(t, int):
                        pe.wait_ge(pt_hi_done[3], now[2])
                        pe.wait_ge(wh_lo[2], now[2])
                    pe.wait_ge(f_full, now[3])
                    layer2_first(0, now[2])
                    if isinstance(t, int):
                        pe.wait_ge(h2t_lo, now[1])
                        pe.wait_ge(wh_lo[2], now[2])
                    pe.wait_ge(z_ready[1], now[1])
                    layer2_first(1, now[2])
                    layer2_last(now[2])
                if stage_b:
                    if isinstance(t, int):
                        pe.wait_ge(pt_lo_done[LAST], now[3])
                        pe.wait_ge(hh_ready[2], now[2])
                        pe.wait_ge(x1_ready, now[1])
                    pe.wait_ge(hh_ready[1], now[2])
                    pe.wait_ge(y_ready, now[3])
                    neighbour_sums(now[0])
                if stage_d:
                    if isinstance(t, int):
                        pe.wait_ge(hh_ready[LAST], now[3])
                        pe.wait_ge(pt_hi_done[1], now[2])
                    pe.wait_ge(hh_ready[3], now[2])
                    rows_of(2, now[2])
                if stage_c:
                    pe.wait_ge(wh_lo[0], now[1])
                    pe.wait_ge(z_ready[0], now[1])
                    features(1, now[1])
                    if isinstance(t, int):
                        pe.wait_ge(f_full, now[3])
                        pe.wait_ge(pt_hi_done[3], now[2])
                        pe.wait_ge(z_ready[1], now[1])
                    pe.wait_ge(w2_lo, now[2])
                    features(2, now[1])
                    if isinstance(t, int):
                        pe.wait_ge(hh_ready[3], now[2])
                        pe.wait_ge(hh_ready[LAST], now[3])
                    pe.wait_ge(z_ready[2], now[2])
                    turn_p(1, now[1])
                    pe.wait_ge(wh_lo[0], now[1])
                    turn_p(2, now[1])
                if stage_d:
                    if isinstance(t, int):
                        pe.wait_ge(hh_ready[1], now[2])
                    pe.wait_ge(g_lo, now[0])
                    turn_p(LAST, now[2])
                if stage_b:
                    pe.wait_ge(g_lo, now[0])
                    first_products(now[0])
                if stage_c:
                    pe.wait_ge(pt_hi_done[2], now[1])
                    turn_p(0, now[1])
                if stage_d:
                    if isinstance(t, int):
                        pe.wait_ge(z_ready[2], now[2])
                    pe.wait_ge(pt_hi_done[1], now[1])
                    head_out(LAST, now[2])
                if stage_c:
                    if isinstance(t, int):
                        pe.wait_ge(g_lo, now[0])
                        pe.wait_ge(y_ready, now[3])
                    pe.wait_ge(x1_ready, now[0])
                    head_out(2, now[1])
                    if isinstance(t, int):
                        pe.wait_ge(g_lo, now[0])
                    pe.wait_ge(pt_lo_done[LAST], now[2])
                    head_out(1, now[1])
                if stage_d:
                    if isinstance(t, int):
                        pe.wait_ge(wh_lo[0], now[1])
                    pe.wait_ge(wh_lo[1], now[1])
                    turn_out(now[2])
                if stage_c:
                    pe.wait_ge(wh_lo[2], now[1])
                    turn_p(3, now[1])
                if stage_b:
                    if isinstance(t, int):
                        pe.wait_ge(w2_lo, now[2])
                        pe.wait_ge(z_ready[1], now[1])
                    pe.wait_ge(wh_lo[2], now[1])
                    turn_h2(now[0])
                if stage_c:
                    pe.wait_ge(wh_lo[1], now[1])
                    head_out(0, now[1])
                if stage_d:
                    if isinstance(t, int):
                        pe.wait_ge(wh_lo[2], now[1])
                        pe.wait_ge(w2_lo, now[2])
                    pe.wait_ge(pt_hi_done[3], now[1])
                    ffn_hidden(now[2])
                if stage_c:
                    if isinstance(t, int):
                        pe.wait_ge(pt_hi_done[1], now[1])
                    pe.wait_ge(hh_ready[LAST], now[2])
                    head_out(3, now[1])

            turns(pe, turn)

        @block.scalar
        def _(act):
            def weights_high(full, s):
                nc.scalar.activation(s[0][:, :, :], full, ACT.Copy).then_inc(high_ready, 1)

            act.wait_ge(setup_psum, 2)
            weights_high(bank[:, BANK_W:BANK_W + 2, :].rearrange("p k (t n) -> p (k t) n", t=2), wij_s)

            def heads_high():
                act.wait_ge(column_ready, 2 * H * DT)
                weights_high(wv, wv_s)

            def late_high():
                act.wait_ge(column_ready, 2 * H * DT + 2 * KT)
                weights_high(wo, wo_s)
                weights_high(w1_f[:, :, :], w1_s)
                weights_high(w2_f[:, :, :], w2_s)

            def turn(t, stage_b, stage_c, stage_d, stage_e):
                now = counts(act, t)

                def ln_relu_1(n, n_last):
                    act.wait_ge(h_lo, n_last)
                    act.wait_ge(bias1, n)
                    for i in range(NT):
                        last = nc.scalar.activation(h_f[:, i, :], x_t[:, i, :], ACT.Relu, bias=nb1[:, i:i + 1],
                                                    scale=rs1[:, i:i + 1])
                    last.then_inc(h_full, 1)

                def ln_relu_2(n, n_last):
                    act.wait_ge(h2t_psum, n_last)
                    act.wait_ge(bias2, n)
                    for i in range(NT):
                        last = nc.scalar.activation(h2[:, i, :], x1a[:, i, :], ACT.Relu, bias=nb2[:, i:i + 1],
                                                    scale=rs2[:, i:i + 1])
                    last.then_inc(h2_ready, 1)

                def ln_last(n, n_last):
                    act.wait_ge(yg_ready, n_last)
                    act.wait_ge(bias3, n)
                    for i in range(NT):
                        last = nc.scalar.activation(yn[:, i, :], y[:, i, :], ACT.Identity, bias=nb3[:, i:i + 1],
                                                    scale=rs3[:, i:i + 1])
                    last.then_inc(yn_ready, 1)

                def sums_high(n):
                    act.wait_ge(sums_psum, n)
                    nc.scalar.activation(g_s[0][:, :, :], bank[:, BANK_SUMS:BANK_SUMS + 2, :], ACT.Copy).then_inc(g_hi, 1)

                def h2t_high(n):
                    act.wait_ge(h2t_psum, n)
                    nc.scalar.activation(h2t_s[0][:, :, :], tiles(BANK_H2T), ACT.Copy).then_inc(h2t_hi, 1)

                def out_high(n):
                    act.wait_ge(ot_psum, n)
                    nc.scalar.activation(ot_s[0][:, :, :], tiles(BANK_OT), ACT.Copy).then_inc(ot_hi, 1)

                def probs(h, n, n_last):
                    act.wait_ge(negm4_ready if h == LAST else negm_ready, n)
                    act.wait_ge(hh_ready[h], n_last)
                    act.wait_ge(rinv_ready[h], n_last)
                    act.wait_ge(leaky_ready[h], n)
                    for i in range(NT):
                        m = negm4[:, i, 0:1] if h == LAST else negm[:, i, h:h + 1]
                        last = nc.scalar.activation(p[h][:, i, :], z[h][:, i, :], ACT.Exp, bias=m,
                                                    accum_out=rsum[h][:, i:i + 1])
                    last.then_inc(p_ready[h], 1)

                def elu_exp(h, n):
                    act.wait_ge(pv_psum[h], n)
                    if h == LAST:
                        act.wait_ge(rinv_ready[h], n)
                        for i in range(NT):
                            last = nc.scalar.activation(p[h][:, i, :], tiles(bank_pv[h])[:, i, :], ACT.Exp,
                                                        scale=rinv[h][:, i:i + 1])
                    else:
                        last = nc.scalar.activation(p[h][:, :, :], tiles(bank_pv[h]), ACT.Exp)
                    last.then_inc(ex_ready[h], 1)

                def hidden(n, n_last):
                    act.wait_ge(late_in, 11 * 16)
                    act.wait_ge(f_lo, n_last)
                    act.wait_ge(f_psum, n)
                    for i in range(DT):
                        last = nc.scalar.activation(ff[:, i, :], tiles(BANK_FF)[:, i, :], ACT.Relu, bias=b1_c[:, i:i + 1])
                    last.then_inc(f_full, 1)

                def h_high(n, n_last):
                    act.wait_ge(sums_psum, n_last)
                    act.wait_ge(h_full, n)
                    nc.scalar.activation(h_s[0][:, :, :], h_f[:, :, :], ACT.Copy).then_inc(h_hi, 1)

                def hidden_high(n, n_last):
                    act.wait_ge(y_psum, n_last)
                    act.wait_ge(f_full, n)
                    nc.scalar.activation(ff_s[0][:, :, :], ff[:, :, :], ACT.Copy).then_inc(f_hi, 1)

                def ht_high(h, n, n_last):
                    act.wait_ge(l2_psum, n_last)
                    act.wait_ge(hh_ready[h], n)
                    nc.scalar.activation(ht_s[0][:, DT * h:DT * h + DT, :], hh[h][:, :, :], ACT.Copy).then_inc(ht_hi[h], 1)

                def pt_high(h, n, n_last):
                    if h == H - 1:
                        act.wait_ge(pv_psum[h], n_last)
                    act.wait_ge(pt_psum[h], n)
                    if h == LAST:
                        nc.scalar.activation(pt_hi[h][:, :, :], tiles(bank_pt[h]), ACT.Copy).then_inc(pt_hi_done[h], 1)
                    else:
                        nc.scalar.activation(pt_hi[h][:, :, :], tiles(bank_pt[h]), ACT.Copy)
                        nc.scalar.activation(p[h][:, :, :], tiles(bank_pt[h]), ACT.Copy).then_inc(pt_hi_done[h], 1)

                def features_high(c, n, n_last):
                    if c == CHUNKS - 1:
                        act.wait_ge(pv_psum[H - 1], n_last)
                    act.wait_ge(f12_ready if c == 0 else wh_psum[c], n)
                    nc.scalar.activation(wh_s[0][:, :, c * CW:(c + 1) * CW], bank[:, bank_wh[c]:bank_wh[c] + 2, 0:CW], ACT.Copy).then_inc(wh_hi[c], 1)

                def add_f1(h, n):
                    act.wait_ge(z_ready[2 if h == LAST else h // 2], n)
                    for i in range(NT):
                        f1 = f12_2[:, i, 0:1] if h == LAST else f12[:, i, h:h + 1]
                        last = nc.scalar.activation(z[h][:, i, :], z[h][:, i, :], ACT.Identity, bias=f1)
                    last.then_inc(e_ready[h], 1)

                def normalise(h, n):
                    act.wait_ge(rinv_ready[h], n)
                    for i in range(NT):
                        last = nc.scalar.activation(p[h][:, i, :], p[h][:, i, :], ACT.Copy, scale=rinv[h][:, i:i + 1])
                    last.then_inc(pn_ready[h], 1)

                if stage_d:
                    ht_high(0, now[2], now[3])
                if stage_c:
                    features_high(0, now[1], now[2])
                if stage_b:
                    ln_relu_1(now[0], now[1])
                if stage_d:
                    ht_high(3, now[2], now[3])
                if stage_b:
                    h_high(now[0], now[1])
                if stage_c:
                    add_f1(1, now[1])
                    add_f1(0, now[1])
                    add_f1(2, now[1])
                    add_f1(3, now[1])
                    probs(1, now[1], now[2])
                    probs(2, now[1], now[2])
                    probs(0, now[1], now[2])
                    normalise(1, now[1])
                if stage_b:
                    sums_high(now[0])
                if isinstance(t, int) and t == 0:
                    heads_high()
                if stage_e:
                    ln_last(now[3], now[4])
                if stage_c:
                    features_high(1, now[1], now[2])
                if stage_d:
                    probs(LAST, now[2], now[3])
                if stage_c:
                    features_high(2, now[1], now[2])
                if stage_d:
                    pt_high(LAST, now[2], now[3])
                if stage_c:
                    pt_high(2, now[1], now[2])
                    pt_high(1, now[1], now[2])
                    probs(3, now[1], now[2])
                    pt_high(0, now[1], now[2])
                if stage_d:
                    elu_exp(LAST, now[2])
                if stage_c:
                    elu_exp(2, now[1])
                if stage_b:
                    ln_relu_2(now[0], now[1])
                if stage_c:
                    elu_exp(1, now[1])
                if stage_d:
                    out_high(now[2])
                if stage_c:
                    pt_high(3, now[1], now[2])
                if stage_b:
                    h2t_high(now[0])
                if isinstance(t, int) and t == 0:
                    late_high()
                if stage_c:
                    elu_exp(0, now[1])
                    ht_high(1, now[1], now[2])
                if stage_d:
                    hidden(now[2], now[3])
                if stage_c:
                    elu_exp(3, now[1])
                if stage_d:
                    hidden_high(now[2], now[3])

            turns(act, turn)

        @block.vector
        def _(dve):
            def setup_degrees():
                dve.wait_ge(adj_in, 16)
                nc.vector.tensor_copy(adj_f[:, :, :], adj_i[:, :, :]).then_inc(adj_cast, 1)
                dve.wait_ge(adj_cast, 1)
                nc.vector.tensor_reduce(deg[:, :], adj_f[:, :, :], AX.X, ALU.add).then_inc(deg_ready, 1)
                dve.wait_ge(l0_in, 2 * 16)
                dve.wait_ge(deg_ready, 1)
                for i in range(NT):
                    nc.vector.tensor_scalar(deg_b[:, i, :], b_l0[:, :], deg[:, i:i + 1], None, ALU.mult).then_inc(deg_b_ready, 1)

            def setup_adjacency():
                dve.wait_ge(ident_ready, 1)
                for i, c in ((0, 0), (1, 640)):
                    nc.vector.tensor_scalar(ad[:, c:c + P], ident[:, :], deg[:, i:i + 1], None, ALU.mult).then_inc(ad_full, 1)
                dve.wait_ge(setup_psum, 1)
                nc.vector.tensor_copy(ad[:, 128:640], bank[:, BANK_ADJ, :]).then_inc(ad_full, 1)
                dve.wait_ge(ad_full, 3)
                nc.vector.tensor_copy(ad_s[0][:, :], ad[:, :]).then_inc(ad_full, 1)
                dve.wait_ge(ad_full, 4)
                nc.vector.tensor_tensor(ad_s[1][:, :], ad[:, :], ad_s[0][:, :].bitcast(F32), ALU.subtract).then_inc(ad_ready, 1)

            def setup_wij():
                nc.vector.tensor_scalar(mask[:, :, :], adj_f[:, :, :], 0.0, MASKED, ALU.is_le, ALU.mult).then_inc(mask_ready, 1)
                dve.wait_ge(setup_psum, 2)
                dve.wait_ge(high_ready, 1)
                nc.vector.tensor_tensor(wij_s[1][:, :, :], bank[:, BANK_W:BANK_W + 2, :].rearrange("p k (t n) -> p (k t) n", t=2),
                                        wij_s[0][:, :, :].bitcast(F32), ALU.subtract).then_inc(wij_ready, 1)

            def column(n, weights, a, dst):
                if n > 1:
                    dve.wait_ge(column_ready, n - 1)
                nc.vector.tensor_tensor_reduce(junk[:, n % 2, :], weights, a, 1.0, 0.0, ALU.mult, ALU.add,
                                               dst).then_inc(column_ready, 1)

            def head_columns(heads):
                dve.wait_ge(heads_in, 16 * (H + 1))
                for h in heads:
                    for f in range(DT):
                        for s in range(2):
                            column((h * DT + f) * 2 + s, wv[:, f, NF + h * D:NF + (h + 1) * D],
                                   a_h[:, h, s * D:(s + 1) * D], wv[:, f, s * H + h:s * H + h + 1])

            def layer2_columns(ks):
                dve.wait_ge(late_in, 11 * 16)
                for k in ks:
                    for s in range(2):
                        column((KT + k) * 2 + s, wo[:, k, 0:D], a_o[:, s * D:(s + 1) * D], wo[:, k, D + s:D + s + 1])

            def turn(t, stage_b, stage_c, stage_d, stage_e):
                now = counts(dve, t)
                loaded = 16 * now[0] if isinstance(t, int) else dve.snap(now[0] * 16)

                def statistics(src, st, stats):
                    for i in range(NT):
                        last = nc.vector.bn_stats(st[:, i, :], src[:, i, :])
                    last.then_inc(stats, 1)

                def moments_of(st, mv, stats, moments, n):
                    dve.wait_ge(x_loaded, 16)
                    dve.wait_ge(stats, n)
                    for i in range(NT):
                        last = nc.vector.bn_aggr(mv[:, i, :], st[:, i, :])
                    last.then_inc(moments, 1)

                def variance(mv, ve, moments, var, n):
                    dve.wait_ge(moments, n)
                    nc.vector.tensor_scalar(ve[:, :], mv[:, :, 1], EPS, None, ALU.add).then_inc(var, 1)

                def shift(nb, mv, rs, rstd, bias, n):
                    dve.wait_ge(rstd, n)
                    nc.vector.scalar_tensor_tensor(out=nb[:, :], in0=mv[:, :, 0], scalar=-1.0, in1=rs[:, :],
                                                   op0=ALU.mult, op1=ALU.mult).then_inc(bias, 1)

                def keep_low(dst, src, hi, hi_done, lo_done, n):
                    dve.wait_ge(hi_done, n)
                    nc.vector.tensor_tensor(dst, src, hi.bitcast(F32), ALU.subtract).then_inc(lo_done, 1)

                def sums_low(n):
                    keep_low(g_s[1][:, :, :], bank[:, BANK_SUMS:BANK_SUMS + 2, :], g_s[0][:, :, :], g_hi, g_lo, n)

                def h2t_low(n):
                    keep_low(h2t_s[1][:, :, :], tiles(BANK_H2T), h2t_s[0][:, :, :], h2t_hi, h2t_lo, n)

                def out_low(n):
                    keep_low(ot_s[1][:, :, :], tiles(BANK_OT), ot_s[0][:, :, :], ot_hi, ot_lo, n)

                def features_low(c, n):
                    keep_low(wh_s[1][:, :, c * CW:(c + 1) * CW], bank[:, bank_wh[c]:bank_wh[c] + 2, 0:CW],
                             wh_s[0][:, :, c * CW:(c + 1) * CW], wh_hi[c], wh_lo[c], n)

                def features2_low(n):
                    keep_low(w2h_s[1][:, :, :], bank[:, BANK_L2:BANK_L2 + 2, 0:D], w2h_s[0][:, :, :], w2_hi, w2_lo, n)

                def keep_f12(n):
                    dve.wait_ge(wh_psum[0], n)
                    nc.vector.tensor_copy(f12[:, :, :], bank[:, bank_wh[0]:bank_wh[0] + 2, 0:NF]).then_inc(f12_ready, 1)

                def keep_f12_2(n):
                    dve.wait_ge(l2_psum, n)
                    nc.vector.tensor_copy(f12_2[:, :, :], bank[:, BANK_L2:BANK_L2 + 2, D:D + 2]).then_inc(f12_2_ready, 1)

                def masked(k, n):
                    dve.wait_ge(mask_ready, 1)
                    dve.wait_ge(rows_psum[k], n)
                    for h, mx, col in ((LAST, m24, 0),) if k == 2 else ((2 * k, m2, 2 * k), (2 * k + 1, m2, 2 * k + 1)):
                        for i in range(NT):
                            last = nc.vector.tensor_tensor_reduce(
                                z[h][:, i, :], tiles(bank_rows[k])[:, h % 2, :], mask[:, i, :], 1.0, -3e38, ALU.add, ALU.max,
                                mx[:, i, col:col + 1])
                    last.then_inc(z_ready[k], 1)

                def maxima_sum(f1, mx, ns, z_done, ns_ready, n):
                    dve.wait_ge(z_done, n)
                    nc.vector.scalar_tensor_tensor(out=ns[:, :, :], in0=mx[:, :, :], scalar=-1.0, in1=f1,
                                                   op0=ALU.mult, op1=ALU.subtract).then_inc(ns_ready, 1)

                def maxima_leaky(ns, nm, ns_ready, nm_ready, n):
                    dve.wait_ge(ns_ready, n)
                    nc.vector.scalar_tensor_tensor(out=nm[:, :, :], in0=ns[:, :, :], scalar=SLOPE, in1=ns[:, :, :],
                                                   op0=ALU.mult, op1=ALU.min).then_inc(nm_ready, 1)

                def leaky(h, n):
                    dve.wait_ge(e_ready[h], n)
                    nc.vector.scalar_tensor_tensor(out=z[h][:, :, :], in0=z[h][:, :, :], scalar=SLOPE, in1=z[h][:, :, :],
                                                   op0=ALU.mult, op1=ALU.max).then_inc(leaky_ready[h], 1)

                def inverse(h, n):
                    dve.wait_ge(p_ready[h], n)
                    nc.vector.reciprocal(rinv[h][:, :], rsum[h][:, :]).then_inc(rinv_ready[h], 1)

                def elu_clip(h, n):
                    dve.wait_ge(ex_ready[h], n)
                    nc.vector.tensor_scalar(p[h][:, :, :], p[h][:, :, :], 1.0, -1.0, ALU.min, ALU.add).then_inc(em_ready[h], 1)

                def elu_max(h, n, n_last):
                    if isinstance(t, int) and t == 1:
                        dve.wait_ge(late_ready, 1)
                    if h == LAST:
                        dve.wait_ge(ob2_ready, n_last)
                        dve.wait_ge(em_ready[h], n)
                        for i in range(NT):
                            last = nc.vector.scalar_tensor_tensor(out=hh[h][:, i, :], in0=tiles(bank_pv[h])[:, i, :],
                                                                  scalar=rinv[h][:, i:i + 1], in1=p[h][:, i, :],
                                                                  op0=ALU.mult, op1=ALU.max)
                    else:
                        dve.wait_ge(ht_lo[h], n_last)
                        dve.wait_ge(em_ready[h], n)
                        last = nc.vector.tensor_tensor(hh[h][:, :, :], tiles(bank_pv[h]), p[h][:, :, :], ALU.max)
                    last.then_inc(hh_ready[h], 1)

                def first_residual(n, n_last):
                    dve.wait_ge(x1_psum, n)
                    dve.wait_ge(xdb_ready, n)
                    dve.wait_ge(h2_ready, n_last)
                    dve.wait_ge(x1_kept, n_last)
                    nc.vector.tensor_tensor(x1a[:, :, :], tiles(BANK_X1), xdb[:, :, :], ALU.add).then_inc(x1_ready, 1)

                def ffn_residual(n, n_last):
                    dve.wait_ge(yn_ready, n_last)
                    dve.wait_ge(ob2_ready, n)
                    dve.wait_ge(y_psum, n)
                    nc.vector.tensor_tensor(y[:, :, :], tiles(BANK_Y), ob2[:, :, :], ALU.add).then_inc(y_ready, 1)

                def ht_high(h, n, n_last):
                    dve.wait_ge(l2_psum, n_last)
                    dve.wait_ge(hh_ready[h], n)
                    nc.vector.tensor_copy(ht_s[0][:, DT * h:DT * h + DT, :], hh[h][:, :, :]).then_inc(ht_hi[h], 1)

                def features2_high(n):
                    dve.wait_ge(f12_2_ready, n)
                    nc.vector.tensor_copy(w2h_s[0][:, :, :], bank[:, BANK_L2:BANK_L2 + 2, 0:D]).then_inc(w2_hi, 1)

                def keep_x1(n, n_last):
                    dve.wait_ge(x1_beta, n_last)
                    dve.wait_ge(x1_ready, n)
                    nc.vector.tensor_copy(x1b[:, :, :], x1a[:, :, :]).then_inc(x1_kept, 1)

                def add_f1(h, n):
                    dve.wait_ge(z_ready[2 if h == LAST else h // 2], n)
                    for i in range(NT):
                        f1 = f12_2[:, i, 0:1] if h == LAST else f12[:, i, h:h + 1]
                        last = nc.vector.tensor_scalar(z[h][:, i, :], z[h][:, i, :], f1, None, ALU.add)
                    last.then_inc(e_ready[h], 1)

                def normalise(h, n):
                    dve.wait_ge(rinv_ready[h], n)
                    for i in range(NT):
                        last = nc.vector.tensor_scalar(p[h][:, i, :], p[h][:, i, :], rinv[h][:, i:i + 1], None, ALU.mult)
                    last.then_inc(pn_ready[h], 1)

                def pt_low(h, n):
                    dve.wait_ge(pt_hi_done[h], n)
                    nc.vector.tensor_tensor(pt_lo[h][:, :, :], tiles(bank_pt[h]), pt_hi[h][:, :, :].bitcast(F32),
                                            ALU.subtract).then_inc(pt_lo_done[h], 1)

                if stage_b:
                    dve.wait_ge(x_loaded, loaded)
                    statistics(x_t, st1, stats1)
                    moments_of(st1, mv1, stats1, moments1, now[0])
                    variance(mv1, ve1, moments1, var1, now[0])
                if isinstance(t, int) and t == 0:
                    setup_degrees()
                if stage_d:
                    elu_clip(3, now[2])
                if stage_c:
                    keep_f12(now[1])
                if stage_d:
                    elu_max(3, now[2], now[3])
                if stage_b:
                    shift(nb1, mv1, rs1, rstd1, bias1, now[0])
                if isinstance(t, int) and t == 0:
                    setup_adjacency()
                    setup_wij()
                    head_columns(range(H))
                if stage_c:
                    masked(0, now[1])
                    masked(1, now[1])
                if stage_e:
                    ffn_residual(now[3], now[4])
                    dve.wait_ge(y_ready, now[3])
                    statistics(y, st3, stats3)
                if stage_c:
                    maxima_sum(f12[:, :, 0:H], m2, nsum, z_ready[1], nsum_ready, now[1])
                    leaky(1, now[1])
                    maxima_leaky(nsum, negm, nsum_ready, negm_ready, now[1])
                    leaky(2, now[1])
                    leaky(0, now[1])
                if stage_e:
                    moments_of(st3, mv3, stats3, moments3, now[3])
                if stage_c:
                    features_low(0, now[1])
                if stage_e:
                    variance(mv3, ve3, moments3, var3, now[3])
                if stage_c:
                    inverse(1, now[1])
                if stage_d:
                    keep_f12_2(now[2])
                if stage_c:
                    inverse(2, now[1])
                if stage_d:
                    features2_high(now[2])
                if stage_e:
                    shift(nb3, mv3, rs3, rstd3, bias3, now[3])
                if stage_c:
                    normalise(2, now[1])
                if stage_d:
                    features2_low(now[2])
                    masked(2, now[2])
                    add_f1(LAST, now[2])
                if stage_c:
                    inverse(0, now[1])
                if stage_d:
                    maxima_sum(f12_2[:, :, 0:1], m24, nsum4, z_ready[2], nsum4_ready, now[2])
                    leaky(LAST, now[2])
                    maxima_leaky(nsum4, negm4, nsum4_ready, negm4_ready, now[2])
                if stage_b:
                    sums_low(now[0])
                if isinstance(t, int) and t == 0:
                    layer2_columns(range(0, KT // 2))
                if stage_c:
                    leaky(3, now[1])
                    normalise(0, now[1])
                    features_low(1, now[1])
                    features_low(2, now[1])
                if stage_d:
                    pt_low(LAST, now[2])
                if stage_c:
                    keep_x1(now[1], now[2])
                if stage_d:
                    inverse(LAST, now[2])
                if stage_b:
                    first_residual(now[0], now[1])
                    dve.wait_ge(x1_ready, now[0])
                    statistics(x1a, st2, stats2)
                if stage_c:
                    inverse(3, now[1])
                if stage_b:
                    moments_of(st2, mv2, stats2, moments2, now[0])
                    variance(mv2, ve2, moments2, var2, now[0])
                if stage_c:
                    normalise(3, now[1])
                if stage_d:
                    elu_clip(LAST, now[2])
                if stage_b:
                    shift(nb2, mv2, rs2, rstd2, bias2, now[0])
                if isinstance(t, int) and t == 0:
                    layer2_columns(range(KT // 2, KT))
                if stage_d:
                    elu_max(LAST, now[2], now[3])
                if stage_c:
                    elu_clip(2, now[1])
                    elu_max(2, now[1], now[2])
                    elu_clip(1, now[1])
                    ht_high(2, now[1], now[2])
                if stage_d:
                    out_low(now[2])
                if stage_c:
                    elu_max(1, now[1], now[2])
                if stage_b:
                    h2t_low(now[0])
                if stage_c:
                    elu_clip(0, now[1])
                    elu_max(0, now[1], now[2])

            turns(dve, turn)


_INS = ['x', 'adj', 'L0_gnn_W', 'L0_gnn_b', 'L1_gnn_W_heads', 'L1_gnn_a_heads', 'L1_gnn_W_out', 'L1_gnn_a_out',
        'L1_gnn_w1', 'L1_gnn_b1', 'L1_gnn_w2', 'L1_gnn_b2', 'L1_gnn_ln_gamma', 'L1_gnn_ln_beta']


def kernel(**inputs):
    import numpy as _np
    import concourse.bacc as _bacc
    from concourse import mybir as _mybir
    from concourse.bass_utils import run_bass_kernel_spmd as _run

    nc = _bacc.Bacc("TRN2", target_bir_lowering=False, num_devices=1)
    arrays, args = {}, []
    for name in _INS:
        a = _np.ascontiguousarray(inputs[name])
        arrays[f"in_{name}_dram"] = a
        args.append(nc.dram_tensor(f"in_{name}_dram", a.shape, _mybir.dt.from_np(a.dtype), kind="ExternalInput").ap())
    shape = inputs['x'].shape
    args.append(nc.dram_tensor("out_0_dram", tuple(shape), _mybir.dt.float32, kind="ExternalOutput").ap())
    gnn_block_kernel(nc, *args)
    r = _run(nc, [arrays], core_ids=[0])
    return r.results[0]["out_0_dram"]
```
